# Optimizing a Trainium2 kernel written in Bass

```python
import numpy as np
import jax
import jax.numpy as jnp

def _softmax(x, axis=-1):
    return jax.nn.softmax(x, axis=axis)

def _gelu(x):
    return jax.nn.gelu(x, approximate=True)

def _silu(x):
    return jax.nn.silu(x)

def _sigmoid(x):
    return jax.nn.sigmoid(x)

def _layernorm(x, axis=-1, eps=1e-05):
    m = jnp.mean(x, axis=axis, keepdims=True)
    v = jnp.var(x, axis=axis, keepdims=True)
    return (x - m) / jnp.sqrt(v + eps)

def _scatter_add(tgt, idx, src, axis=0):
    return tgt.at[idx].add(src)

def _segment_sum(src, seg, n):
    return jax.ops.segment_sum(src, seg, n)
kernel_name = 'mk_xattn_ffn_d1_seqx_r4_30ac66'

def setup_inputs(seed: int=0):
    np.random.seed(seed)
    _w = jnp.asarray

    def _rec_inputs():
        import jax
        import jax.numpy as jnp
        _rk = jax.random.key(seed)
        x = 7.22e-05 + 1 * jax.random.normal(jax.random.fold_in(_rk, 1), (16, 512, 256), jnp.float32)
        _lenS = 512 - jax.random.randint(jax.random.fold_in(_rk, 7), (16,), 0, max(1, 512 // 4) + 1, jnp.int32)
        _lenS2 = 1601 - jax.random.randint(jax.random.fold_in(_rk, 8), (16,), 0, max(1, 1601 // 4) + 1, jnp.int32)
        _ctx_1024P = jax.random.normal(jax.random.fold_in(_rk, 11), (16, 16, 256), jnp.float32)
        _ctx_1024c = jax.random.dirichlet(jax.random.fold_in(_rk, 511), 0.3 * jnp.ones((16,), jnp.float32), (16, 1601))
        _ctx_1024t = jnp.einsum('bsk,bkd->bsd', _ctx_1024c, _ctx_1024P)
        _ctx_1024t = _ctx_1024t * jax.lax.rsqrt(jnp.mean(jnp.square(_ctx_1024t)) + 1e-12) * 0.953939
        ctx_1024 = 2.81802e-05 + 1.00001 * (_ctx_1024t + 0.3 * jax.random.normal(jax.random.fold_in(_rk, 611), (16, 1601, 256), jnp.float32))
        return (x, ctx_1024)
    x, ctx_1024 = _rec_inputs()

    def _L0_xattn_setup():
        import jax, jax.numpy as jnp
        import numpy as np
        B, T, S, D = (4, 512, 1024, 256)
        TOP_K = 32

        def _read(query, mem_state, top_k, Wq, bq, Wk, bk, Wv, bv, Wo, bo):
            b, t, d = query.shape
            s = mem_state.shape[1]
            scale = 1.0 / np.sqrt(d)
            q = query @ Wq.T + bq
            k = mem_state @ Wk.T + bk
            v = mem_state @ Wv.T + bv
            scores = jnp.einsum('btd,bsd->bts', q, k) * scale
            if top_k < s:
                vals, idx = jax.lax.top_k(scores, top_k)
                b_ix = jnp.arange(b)[:, None, None]
                t_ix = jnp.arange(t)[None, :, None]
                masked = jnp.full_like(scores, -jnp.inf)
                scores = masked.at[b_ix, t_ix, idx].set(vals)
            attn = jax.nn.softmax(scores, axis=-1)
            ctx = jnp.einsum('bts,bsd->btd', attn, v)
            return ctx @ Wo.T + bo
        key = jax.random.key(seed)
        ks = jax.random.split(key, 12)
        std = 0.02
        inp = {'query': jax.random.normal(ks[0], (B, T, D), dtype=jnp.float32), 'mem_state': jax.random.normal(ks[1], (B, S, D), dtype=jnp.float32), 'top_k': TOP_K, 'Wq': jax.random.normal(ks[2], (D, D), dtype=jnp.float32) * std, 'bq': jnp.zeros((D,), dtype=jnp.float32), 'Wk': jax.random.normal(ks[3], (D, D), dtype=jnp.float32) * std, 'bk': jnp.zeros((D,), dtype=jnp.float32), 'Wv': jax.random.normal(ks[4], (D, D), dtype=jnp.float32) * std, 'bv': jnp.zeros((D,), dtype=jnp.float32), 'Wo': jax.random.normal(ks[5], (D, D), dtype=jnp.float32) * std, 'bo': jnp.zeros((D,), dtype=jnp.float32)}
        return inp
    _L0_xattn_all = _L0_xattn_setup()
    _L0_xattn_in = {k: v for k, v in _L0_xattn_all.items() if k in ('Wq', 'bq', 'Wk', 'bk', 'Wv', 'bv', 'Wo', 'bo')}
    del _L0_xattn_all

    def _L0_ffn_setup():
        import jax, jax.numpy as jnp
        import numpy as np
        B, S, D = (2, 512, 256)
        E, K, F = (16, 2, 128)
        FS = 256
        key = jax.random.key(seed)
        ks = jax.random.split(key, 8)

        def w(k, shape, fan_in):
            return jax.random.normal(k, shape, jnp.float32) / np.sqrt(fan_in).astype(np.float32)
        return {'x': jax.random.normal(ks[0], (B, S, D), jnp.float32), 'Wr': w(ks[1], (D, E), D), 'Wg': w(ks[2], (E, D, F), D), 'Wu': w(ks[3], (E, D, F), D), 'Wd': w(ks[4], (E, F, D), F), 'Sg': w(ks[5], (D, FS), D), 'Su': w(ks[6], (D, FS), D), 'Sd': w(ks[7], (FS, D), FS)}
    _L0_ffn_all = _L0_ffn_setup()
    _L0_ffn_in = {k: v for k, v in _L0_ffn_all.items() if k in ('Wr', 'Wg', 'Wu', 'Wd', 'Sg', 'Su', 'Sd')}
    del _L0_ffn_all
    return {'x': x, 'ctx_1024': ctx_1024, 'L0_xattn_Wq': _L0_xattn_in['Wq'], 'L0_xattn_bq': _L0_xattn_in['bq'], 'L0_xattn_Wk': _L0_xattn_in['Wk'], 'L0_xattn_bk': _L0_xattn_in['bk'], 'L0_xattn_Wv': _L0_xattn_in['Wv'], 'L0_xattn_bv': _L0_xattn_in['bv'], 'L0_xattn_Wo': _L0_xattn_in['Wo'], 'L0_xattn_bo': _L0_xattn_in['bo'], 'L0_ffn_Wr': _L0_ffn_in['Wr'], 'L0_ffn_Wg': _L0_ffn_in['Wg'], 'L0_ffn_Wu': _L0_ffn_in['Wu'], 'L0_ffn_Wd': _L0_ffn_in['Wd'], 'L0_ffn_Sg': _L0_ffn_in['Sg'], 'L0_ffn_Su': _L0_ffn_in['Su'], 'L0_ffn_Sd': _L0_ffn_in['Sd']}

def reference(x, ctx_1024, L0_xattn_Wq, L0_xattn_bq, L0_xattn_Wk, L0_xattn_bk, L0_xattn_Wv, L0_xattn_bv, L0_xattn_Wo, L0_xattn_bo, L0_ffn_Wr, L0_ffn_Wg, L0_ffn_Wu, L0_ffn_Wd, L0_ffn_Sg, L0_ffn_Su, L0_ffn_Sd):
    import jax
    import jax.numpy as jnp

    def _L0_xattn_ref(query, mem_state, top_k, Wq, bq, Wk, bk, Wv, bv, Wo, bo):
        import jax, jax.numpy as jnp
        import numpy as np
        B, T, S, D = (4, 512, 1024, 256)
        TOP_K = 32

        def _read(query, mem_state, top_k, Wq, bq, Wk, bk, Wv, bv, Wo, bo):
            b, t, d = query.shape
            s = mem_state.shape[1]
            scale = 1.0 / np.sqrt(d)
            q = query @ Wq.T + bq
            k = mem_state @ Wk.T + bk
            v = mem_state @ Wv.T + bv
            scores = jnp.einsum('btd,bsd->bts', q, k) * scale
            if top_k < s:
                vals, idx = jax.lax.top_k(scores, top_k)
                b_ix = jnp.arange(b)[:, None, None]
                t_ix = jnp.arange(t)[None, :, None]
                masked = jnp.full_like(scores, -jnp.inf)
                scores = masked.at[b_ix, t_ix, idx].set(vals)
            attn = jax.nn.softmax(scores, axis=-1)
            ctx = jnp.einsum('bts,bsd->btd', attn, v)
            return ctx @ Wo.T + bo
        return _read(query, mem_state, top_k, Wq, bq, Wk, bk, Wv, bv, Wo, bo)

    def _L0_ffn_ref(x, Wr, Wg, Wu, Wd, Sg, Su, Sd):
        import jax, jax.numpy as jnp
        import numpy as np
        B, S, D = (2, 512, 256)
        E, K, F = (16, 2, 128)
        FS = 256
        b, s, d = x.shape
        T = b * s
        xf = x.reshape(T, d)
        shared = jax.nn.silu(xf @ Sg) * (xf @ Su) @ Sd
        probs = jax.nn.softmax(xf @ Wr, axis=-1)
        topk_p, topk_i = jax.lax.top_k(probs, K)
        n_exp = Wr.shape[1]
        cw = jnp.zeros((T, n_exp), x.dtype).at[jnp.arange(T)[:, None], topk_i].add(topk_p)

        def step(acc, ew):
            wg, wu, wd, c = ew
            y = jax.nn.silu(xf @ wg) * (xf @ wu) @ wd
            return (acc + y * c[:, None], None)
        routed, _ = jax.lax.scan(step, jnp.zeros_like(xf), (Wg, Wu, Wd, cw.T))
        return (routed + shared).reshape(b, s, d)
    x = x + _L0_xattn_ref(_layernorm(x, axis=-1), ctx_1024, 32, L0_xattn_Wq, L0_xattn_bq, L0_xattn_Wk, L0_xattn_bk, L0_xattn_Wv, L0_xattn_bv, L0_xattn_Wo, L0_xattn_bo)
    x = x + _L0_ffn_ref(_layernorm(x, axis=-1), L0_ffn_Wr, L0_ffn_Wg, L0_ffn_Wu, L0_ffn_Wd, L0_ffn_Sg, L0_ffn_Su, L0_ffn_Sd)
    return x

_drawn_inputs = setup_inputs


def setup_inputs(seed=0):
    import zlib

    import numpy as np

    out = dict(_drawn_inputs(seed))
    spreads = {'L0_xattn_bq': (0.0, 0.1),
     'L0_xattn_bk': (0.0, 0.1),
     'L0_xattn_bv': (0.0, 0.1),
     'L0_xattn_bo': (0.0, 0.1)}
    factors = {}
    for name, (base, spread) in spreads.items():
        noise = np.random.default_rng([zlib.crc32(name.encode()), seed]).standard_normal(out[name].shape)
        drawn = base * np.exp(spread * noise) if base else spread * noise
        out[name] = jnp.asarray(drawn.astype(out[name].dtype))
    for name, factor in factors.items():
        out[name] = (out[name] * factor).astype(out[name].dtype)
    return out
```

```python
from contextlib import ExitStack

import concourse.bass as bass
from concourse import mybir

P = 128
F32 = mybir.dt.float32
BF16 = mybir.dt.bfloat16
I32 = mybir.dt.int32
U32 = mybir.dt.uint32
ALU = mybir.AluOpType
ACT = mybir.ActivationFunctionType
AX_X = mybir.AxisListType.X

TOP_K = 32
ROUNDS = TOP_K // 8
LN_EPS = 1e-5
GONE = -3.0e38
TPB = 4


class Count:

    def __init__(self):
        self.base, self.n = 0, 0

    def next(self):
        self.n += 1
        return self.now()

    def now(self, back=0):
        return self.base + (self.n - back)

    def at(self, base):
        self.base, self.n = base, 0


def since(v, first):
    return not isinstance(v, int) or v >= first


def live(v, lag, n):
    return not isinstance(v, int) or 0 <= v - lag < n


def xattn_moe_kernel(nc, x, ctx_1024, Wq, bq, Wk, bk, Wv, bv, Wo, bo, Wr, Wg, Wu, Wd, Sg, Su, Sd, out):
    B, T, D = x.shape
    S = ctx_1024.shape[1]
    E, _, F = Wg.shape
    FS = Sg.shape[1]
    DC = D // P
    FC = FS // P
    NT = B * T // P
    SF = S // P
    SR = S - SF * P
    SC = SF + 1
    SCALE = float(D) ** -0.5
    assert T == TPB * P and D == 2 * P and F == P and FS == 2 * P and B % 2 == 0 and B >= 6 and 0 < SR < P
    EROWS = B * T + P
    MT = 2 * NT + E
    RING = 8
    assert MT % RING == 0
    GROUPS = [list(range(g, min(g + 4, SC))) for g in range(0, SC, 4)]
    NG = len(GROUPS)
    CHUNKS = [(c, min(c + 512, S)) for c in range(0, S, 512)]
    TK = 2 * ROUNDS
    RK = 19
    PREP_TURNS = DC * NG + 2 * DC + 1
    BATCH_TURNS = TPB * (NG + 1) + PREP_TURNS + DC + 1 + 2 * FC + TPB // 2 + 1

    def rows(c):
        return P if c < SF else SR

    x_t = x.rearrange("b (j p) d -> p (b j) d", p=P)
    out_t = out.rearrange("b (j p) d -> p (b j) d", p=P)

    with ExitStack() as ctx:
        def sb(name, shape, dt=F32):
            return ctx.enter_context(nc.sbuf_tensor(name, shape, dt))

        def psum(name, shape, dt=F32):
            return ctx.enter_context(nc.psum_tensor(name, shape, dt))

        def sem(name):
            return ctx.enter_context(nc.semaphore(name))

        expert_in = nc.dram_tensor("expert_in", [E * EROWS, D], F32, kind="Internal").ap()
        expert_out = nc.dram_tensor("expert_out", [MT * P, D], F32, kind="Internal").ap()

        res = sb("res", [P, NT, D])
        mem = sb("mem", [P, 2, SC, D + 1])
        memT = sb("memT", [P, 2, DC, S])
        work = sb("work", [P, 5, S])
        score, rest, prob = work[:, 0:2, :], work[:, 2:4, :], work[:, 4, :]
        probT = sb("probT", [P, SC, P])
        qT = sb("qT", [P, DC, T])
        xnT = sb("xnT", [P, DC, T])
        xn = sb("xn", [P, TPB, D])
        xn2 = sb("xn2", [P, 2, TPB, D])
        xn2T = sb("xn2T", [P, DC, T])
        gateact = sb("gateact", [P, 3, T])
        hid = sb("hid", [P, FC, T])
        down = gateact[:, 0:2, :].rearrange("p c (h d) -> p (c h) d", h=2)
        att = sb("att", [P, 2, D + 1])
        attT = sb("attT", [P, DC, P])
        best = sb("best", [P, 2, 8 * ROUNDS])
        negmax = sb("negmax", [P, 2])
        rowc = sb("rowc", [P, TPB])
        rsum = sb("rsum", [P, 2])
        stats = sb("stats", [P, TPB, 6])
        meanvar = sb("meanvar", [P, TPB, 2])
        rstd = sb("rstd", [P, TPB])
        stats2 = sb("stats2", [P, TPB, 6])
        meanvar2 = sb("meanvar2", [P, TPB, 2])
        rstd2 = sb("rstd2", [P, TPB])
        eps = sb("eps", [P, TPB])
        minus_half = sb("minus_half", [P, TPB])
        ident = sb("ident", [P, P])
        before = sb("before", [P, P])
        ones = sb("ones", [P, P])
        iotaE = sb("iotaE", [P, E])
        ebase = sb("ebase", [P, E])
        Sgu_sb = sb("Sgu_sb", [P, DC, 2 * FS])
        Sd_sb = sb("Sd_sb", [P, FC, D])
        Wr_sb = sb("Wr_sb", [P, DC, E])
        Aqk = sb("Aqk", [P, DC, D])
        Cvo = sb("Cvo", [P, DC, D])
        bcols = sb("bcols", [P, 3, DC])
        a_bias = sb("a_bias", [P, DC])
        w_rowc = sb("w_rowc", [P, DC])
        rowc0 = sb("rowc0", [P, 1])
        out_bias = sb("out_bias", [P, D])
        logit = sb("logit", [P, TPB, E])
        lneg = sb("lneg", [P, TPB])
        rexp = sb("rexp", [P, TPB, E])
        rexps = sb("rexps", [P, TPB])
        rinv = sb("rinv", [P, TPB])
        rtop = sb("rtop", [P, TPB, 8])
        ridx = sb("ridx", [P, TPB, 8], U32)
        chosen = sb("chosen", [P, TPB, E])
        cum = sb("cum", [P, TPB + 1, E])
        rank = sb("rank", [P, TPB, E])
        onehot = sb("onehot", [P, TPB, 2, E])
        choice = sb("choice", [P, NT, 2])
        slot = sb("slot", [P, NT, 2])
        gates = sb("gates", [P, NT, 2])
        slot_i = sb("slot_i", [P, 2, TPB, 2], I32)
        tiles_i = sb("tiles_i", [P, E], I32)
        gidx = sb("gidx", [P, TPB, 2], I32)
        pad_i = sb("pad_i", [P, E], I32)
        iota_p = sb("iota_p", [P, 1])

        def weight(buf, i, w):
            return buf[:, i, w * DC * D:(w + 1) * DC * D].rearrange("p (c n) -> p c n", c=DC)

        Wq_sb, Wk_sb, Wv_sb, Wo_sb = weight(work, 2, 0), weight(work, 2, 1), weight(work, 2, 2), weight(work, 3, 0)
        WoT_sb = weight(work, 4, 0)
        brows, bo_row = work[0:3 * DC, 0, 0:P], work[0:1, 1, 0:D]
        bq_wide, bv_wide = (work[:, 4, (2 + i) * DC * P + D:(3 + i) * DC * P + D].rearrange("p (c n) -> p c n", c=DC)
                            for i in range(2))

        scoreP = psum("scoreP", [P, 2048])
        turnP = [psum(f"turnP{i}", [P, 512]) for i in range(2)]
        pvP = psum("pvP", [P, 512])
        outP = psum("outP", [P, 512])

        SETUP_COPIES = 7
        NWEIGHTS = 16 * 4
        PLAN = 21 + 2 * 4

        flat_mem, flat_memT, flat_work = (mem[:].rearrange("p a c d -> p (a c d)"), memT[:].rearrange("p a c s -> p (a c s)"),
                                          work[:].rearrange("p a s -> p (a s)"))
        at = [0]

        def reuse(of, n):
            at[0] += n
            assert at[0] <= of.shape[1]
            return of[:, at[0] - n:at[0]]

        Wgu1_sb = reuse(flat_mem, E * 2 * F).rearrange("p (e f) -> p e f", e=E)
        xin = reuse(flat_mem, RING * D).rearrange("p (r d) -> p r d", r=RING)
        zero_rows = reuse(flat_mem, D)
        at[0] = 0
        Wd_sb = reuse(flat_memT, E * D).rearrange("p (e d) -> p e d", e=E)
        passed = reuse(flat_memT, MT * E).rearrange("p (t e) -> p t e", e=E)
        at[0] = 0
        Wgu0_sb = reuse(flat_work, E * 2 * F).rearrange("p (e f) -> p e f", e=E)
        shifted = reuse(flat_work, 2 * NT * E).rearrange("p (t e) -> p t e", e=E)
        count, tiles, incl0, incl1, excl, shift, gap, padf = (reuse(flat_work, E) for _ in range(8))
        lastt, yrow, tidx, trow = (reuse(flat_work, n) for n in (1, 2 * NT, MT, MT))
        at[0] = E * 2 * F
        gath = reuse(flat_work, TPB * 2 * D).rearrange("p (r k d) -> p r k d", r=TPB, k=2)
        yout = reuse(flat_work, RING // 2 * D).rearrange("p (r d) -> p r d", r=RING // 2)
        incl = [incl0, incl1]
        Wgu_sb = [Wgu0_sb, Wgu1_sb]
        xinT = qT[:].rearrange("p c t -> p (c t)")[:, 0:2 * D].rearrange("p (q c n) -> p q c n", q=2, c=DC)
        etanh, ehid, ehidT = (xnT[:, 0, 0:2 * P].rearrange("p (q n) -> p q n", q=2),
                              xnT[:, 0, 2 * P:4 * P].rearrange("p (q n) -> p q n", q=2),
                              xnT[:, 1, 0:2 * P].rearrange("p (q n) -> p q n", q=2))
        flat_probT = probT[:].rearrange("p c n -> p (c n)")
        at[0] = 0
        iota_t = reuse(flat_probT, MT)
        yrow_i = reuse(flat_probT, 2 * NT).bitcast(I32).rearrange("p (t k) -> p t k", k=2)
        tile_row, tile_expert = (reuse(flat_probT, MT).bitcast(I32) for _ in range(2))
        guP = [scoreP[:, 512 * i:512 * i + 512] for i in range(2)]
        ehTP = [scoreP[:, 512 * i:512 * i + 512] for i in range(2, 4)]
        yP = [pvP, outP]

        s_small = sem("small_loaded")
        s_weights = sem("ffn_weights_loaded")
        s_x = sem("x_loaded")
        s_late = sem("late_weights_loaded")
        s_mem = [sem(f"mem_loaded{i}") for i in range(2)]
        s_const = sem("constants_made")
        s_wide = sem("wide_biases")
        s_bcol = sem("bias_columns")
        s_setup_p = sem("setup_product")
        s_setup_c = sem("setup_copied")
        s_scored = sem("scores_in_psum")
        s_score = sem("scores_copied")
        s_topk = sem("topk_step")
        s_neg = sem("negmax_ready")
        s_exp = sem("exps_done")
        s_masked = sem("prob_masked")
        s_turn = sem("turned")
        s_turnread = sem("turn_read")
        s_pv = sem("pv_done")
        s_att = sem("att_copied")
        s_proj = sem("proj_done")
        s_rsum = sem("rsum_ready")
        s_res = sem("residual_added")
        s_ln = sem("ln1_stats")
        s_lnp = sem("ln1_rstd")
        s_xn = sem("xn_ready")
        s_bias = sem("bias_added")
        s_ln2 = sem("ln2_stats")
        s_ln2p = sem("ln2_rstd")
        s_xn2 = sem("xn2_ready")
        s_logit = sem("logits_copied")
        s_rankc = sem("down_and_ranks_copied")
        s_route = sem("route_step")
        s_rexp = sem("route_exp")
        s_cum = sem("cum_step")
        s_scat = [sem(f"rows_scattered{i}") for i in range(2)]
        s_sact = sem("shared_act")
        s_hid = sem("hidden_step")
        s_shared = sem("shared_added")
        s_held = {k: sem(f"held_{k}") for k in ("pool", "dve")}
        s_count = sem("counts_summed")
        s_plan = sem("plan_step")
        s_iota = sem("tile_numbers_made")
        s_zero = sem("zero_rows_made")
        s_pad = sem("pad_rows_written")
        s_ein = [sem(f"expert_rows_loaded{i}") for i in range(RING)]
        s_eturn = sem("expert_rows_turned")
        s_eturnc = sem("expert_rows_copied")
        s_gu = sem("gate_up_done")
        s_eact = sem("expert_tanh")
        s_eh = sem("expert_hidden_step")
        s_ehT = sem("expert_hidden_turned")
        s_ehTc = sem("expert_hiddenT_copied")
        s_ydone = sem("expert_out_product")
        s_y = sem("expert_out_copied")
        s_ystore = [sem(f"expert_out_stored{i}") for i in range(RING)]
        s_gidx = sem("gather_rows_ready")
        s_gath = [sem(f"rows_gathered{i}") for i in range(TPB)]
        s_final = sem("final_step")
        s_out = sem("out_stored")

        block = ctx.enter_context(nc.Block())

        PAIR = 2 * TPB
        NP = B // 2

        def walk(eng, step, turn=None):
            for t in range(PAIR):
                step(t, t // TPB, t % TPB, t // TPB % 2)
            if turn:
                first, per = turn.n, 2 * BATCH_TURNS
                assert first % 2 == 0 and per % 2 == 0
            with eng.Fori(1, NP - 1) as p:
                if turn:
                    turn.at(p * per + (first - per))
                for j in range(PAIR):
                    step(p * PAIR + j, p * 2 + j // TPB, j % TPB, j // TPB)
                assert turn is None or turn.n == per
            if turn:
                turn.at((NP - 2) * per + first)
            for t in range(NT - PAIR, NT + 2 * TPB):
                step(t, t // TPB, t % TPB, t // TPB % 2)

        def ewalk(eng, step):
            for i in range(RING):
                step(i, i)
            with eng.Fori(1, MT // RING) as p:
                for r in range(RING):
                    step(p * RING + r, r)
            for i in range(MT, MT + 5):
                step(i, i % RING)

        @block.sync
        def _(sp):
            def load_x(b):
                sp.dma_start(res[:, bass.ds(b * TPB, TPB), :], x_t[:, bass.ds(b * TPB, TPB), :]).then_inc(s_x, 16)

            def load_mem(b, par):
                src = ctx_1024[bass.ds(b, 1), :, :]
                sp.dma_start(mem[:, par, 0:SF, 0:D],
                             src[:, 0:SF * P, :].rearrange("a (c p) d -> p (a c) d", p=P)).then_inc(s_mem[par], 16)
                sp.dma_start(mem[0:SR, par, SF, 0:D],
                             src[:, SF * P:S, :].rearrange("a p d -> p (a d)")).then_inc(s_mem[par], 16)

            load_x(0)
            for w_sb, w in ((Wq_sb, Wq), (Wk_sb, Wk), (Wv_sb, Wv), (Wo_sb, Wo)):
                sp.dma_start(w_sb, w.rearrange("(c p) n -> p c n", p=P)).then_inc(s_small, 16)
            for n, bias in enumerate((bq, bk, bv)):
                sp.dma_start(brows[n * DC:(n + 1) * DC, :], bias.rearrange("(c p) -> c p", p=P)).then_inc(s_small, 16)
            sp.dma_start(bo_row[:, :], bo.rearrange("(a n) -> a n", a=1)).then_inc(s_small, 16)
            load_mem(0, 0)
            sp.wait_ge(s_x, 16)
            load_x(1)
            load_mem(1, 1)
            sp.dma_start(Wr_sb[:], Wr.rearrange("(c p) e -> p c e", p=P)).then_inc(s_weights, 16)
            sp.dma_start(Sgu_sb[:, :, 0:FS], Sg.rearrange("(c p) f -> p c f", p=P)).then_inc(s_weights, 16)
            sp.dma_start(Sgu_sb[:, :, FS:2 * FS], Su.rearrange("(c p) f -> p c f", p=P)).then_inc(s_weights, 16)
            sp.dma_start(Sd_sb[:], Sd.rearrange("(c p) d -> p c d", p=P)).then_inc(s_weights, 16)

            def load_gate_up(c, done):
                for w, src in enumerate((Wg, Wu)):
                    for e in range(0, E, E // 2):
                        sp.dma_start(Wgu_sb[c][:, e:e + E // 2, w * F:(w + 1) * F],
                                     src[e:e + E // 2, c * P:(c + 1) * P, :].rearrange("e p f -> p e f")).then_inc(done, 16)
            with sp.Fori(1, NP) as p:
                for par in range(2):
                    b = p * 2 + par
                    sp.wait_ge(s_x, b * 16)
                    load_x(b)
                    sp.wait_ge(s_pv, b * TPB - TPB)
                    load_mem(b, par)

            sp.wait_ge(s_scored, NT)
            sp.wait_ge(s_pv, NT)
            load_gate_up(1, s_late)
            load_gate_up(0, s_late)
            sp.dma_start(Wd_sb[:], Wd.rearrange("e p d -> p e d")).then_inc(s_late, 16)

            for q in range(2):
                sp.wait_ge(s_scat[q], NP * TPB * 2 * 16)
            sp.wait_ge(s_pad, E * 16)
            sp.wait_ge(s_plan, PLAN)

            def load_rows(i, r):
                row = sp.value_load(tile_row[0:1, bass.ds(i, 1)], min_val=0, max_val=(E - 1) * EROWS + B * T)
                sp.dma_start(xin[:, r, :], expert_in[bass.ds(row, P), :]).then_inc(s_ein[r], 16)

            for i in range(RING):
                load_rows(i, i)
            with sp.Fori(1, MT // RING) as p:
                for r in range(RING):
                    sp.wait_ge(s_eturn, p * RING + (r + 1 - RING))
                    load_rows(p * RING + r, r)
            with sp.Fori(0, NT // TPB) as p:
                for r in range(TPB):
                    sp.wait_ge(s_final, p * (2 * TPB) + 2 * (r + 1))
                    sp.dma_start(out_t[:, bass.ds(p * TPB + r, 1), :], res[:, bass.ds(p * TPB + r, 1), :]).then_inc(s_out, 16)
            sp.wait_ge(s_out, NT * 16)

        @block.gpsimd
        def _(pool):
            nc.gpsimd.memset(ident[:], 0.0).then_inc(s_const, 1)
            nc.gpsimd.memset(ones[:], 1.0).then_inc(s_const, 1)
            nc.gpsimd.memset(eps[:], LN_EPS).then_inc(s_const, 1)
            nc.gpsimd.memset(minus_half[:], -0.5).then_inc(s_const, 1)
            nc.gpsimd.memset(cum[:], 0.0).then_inc(s_const, 1)
            nc.gpsimd.memset(mem[:, :, :, D:D + 1], 1.0).then_inc(s_const, 1)
            nc.gpsimd.iota(iotaE[:], pattern=[[1, E]], base=0, channel_multiplier=0,
                           allow_small_or_imprecise_dtypes=True).then_inc(s_const, 1)
            nc.gpsimd.iota(ebase[:], pattern=[[EROWS, E]], base=0, channel_multiplier=0,
                           allow_small_or_imprecise_dtypes=True).then_inc(s_const, 1)
            nc.gpsimd.iota(iota_p[:], pattern=[[0, 1]], base=0, channel_multiplier=1,
                           allow_small_or_imprecise_dtypes=True).then_inc(s_const, 1)
            pool.wait_ge(s_const, 9)
            nc.gpsimd.affine_select(out=ident[:], in_=ident[:], compare_op=ALU.not_equal, fill=1.0, base=0,
                                    pattern=[[-1, P]], channel_multiplier=1).then_inc(s_const, 1)
            nc.gpsimd.affine_select(out=before[:], in_=ones[:], compare_op=ALU.is_ge, fill=0.0, base=-1,
                                    pattern=[[1, P]], channel_multiplier=-1).then_inc(s_const, 1)

            def rstd_of(mv, to, stats_sem, n, done, k):
                pool.wait_ge(stats_sem, n)
                nc.gpsimd.tensor_tensor(to[:], mv[:, :, 1], eps[:], ALU.add).then_inc(done, 1)
                pool.wait_ge(done, k)
                nc.gpsimd.tensor_tensor(to[:], to[:], minus_half[:], ALU.pow).then_inc(done, 1)

            def add_bias(b):
                pool.wait_ge(s_xn, b * TPB + TPB)
                rb = res[:, bass.ds(b * TPB, TPB), :]
                nc.gpsimd.tensor_tensor(rb, rb, out_bias[:, None, :].to_broadcast([P, TPB, D]), ALU.add).then_inc(s_bias, 1)

            rstd_of(meanvar, rstd, s_ln, 2 * TPB, s_lnp, 1)
            pool.wait_ge(s_setup_c, SETUP_COPIES)
            add_bias(0)

            def step(t, b, j, par):
                if j == 3 and live(b, 2, B):
                    c0 = b * 5 - 10
                    pool.wait_ge(s_route, b * RK - 2 * RK + 15)
                    for n in range(TPB):
                        if n or since(b, 3):
                            pool.wait_ge(s_cum, c0 + n)
                        nc.gpsimd.tensor_tensor(cum[:, n + 1, :], cum[:, n, :], chosen[:, n, :], ALU.add).then_inc(s_cum, 1)
                if live(t, 1, NT):
                    q = (j - 1) % 2
                    pool.wait_ge(s_exp, t * 2)
                    nc.gpsimd.tensor_tensor(prob, prob, rest[:, q, :], ALU.subtract).then_inc(s_masked, 1)
                if j == 0 and live(b, -1, B):
                    rstd_of(meanvar, rstd, s_ln, b * 8 + 16, s_lnp, b * 2 + 3)
                if j == 2 and live(b, -1, B):
                    add_bias(b + 1)
                if j == 3 and live(b, 1, B):
                    rstd_of(meanvar2, rstd2, s_ln2, b * 8, s_ln2p, b * 2 - 1)
                if j in (1, 2) and live(b, 2, B):
                    h = j - 1
                    n0 = b * 6 - 12 + 3 * h
                    pool.wait_ge(s_sact, b * 2 - 4 + h + 1)
                    nc.gpsimd.tensor_tensor(gateact[:, 0, :], gateact[:, 0, :], gateact[:, 1, :], ALU.mult).then_inc(s_hid, 1)
                    pool.wait_ge(s_hid, n0 + 1)
                    nc.gpsimd.tensor_tensor(gateact[:, 0, :], gateact[:, 0, :], gateact[:, 1, :], ALU.add).then_inc(s_hid, 1)
                    pool.wait_ge(s_hid, n0 + 2)
                    if since(b, 3):
                        pool.wait_ge(s_rankc, b - 2)
                    nc.gpsimd.tensor_tensor(hid[:, h, :], gateact[:, 0, :], gateact[:, 2, :], ALU.mult).then_inc(s_hid, 1)
                if j == 3 and live(b, 2, B):
                    c0 = b * 5 - 10
                    pool.wait_ge(s_cum, c0 + TPB)
                    pool.wait_ge(s_rankc, b - 1)
                    pool.sem_inc(s_held["pool"], 1)
                    nc.gpsimd.tensor_copy(cum[:, 0, :], cum[:, TPB, :]).then_inc(s_cum, 1)
                    pool.wait_ge(s_route, b * RK - RK)
                    pool.sem_inc(s_held["pool"], 1)
                    for n in range(TPB):
                        for k in range(2):
                            nc.gpsimd.indirect_dma_start(
                                out=expert_in[:, :], out_offset=bass.IndirectOffsetOnAxis(ap=slot_i[:, par, n, k:k + 1], axis=0),
                                in_=xn2[:, par, n, :], in_offset=None).then_inc(s_scat[par], 16)
                    pool.wait_ge(s_rankc, b - 1)
                    rb = res[:, bass.ds(b * TPB - 2 * TPB, TPB), :]
                    nc.gpsimd.tensor_tensor(rb, rb, down[:], ALU.add).then_inc(s_shared, 1)

            walk(pool, step)

            pool.wait_ge(s_pv, NT)
            nc.gpsimd.iota(iota_t, pattern=[[1, MT]], base=0, channel_multiplier=0,
                           allow_small_or_imprecise_dtypes=True).then_inc(s_iota, 1)
            pool.wait_ge(s_zero, 1)
            pool.wait_ge(s_plan, PLAN)
            for e in range(E):
                nc.gpsimd.indirect_dma_start(
                    out=expert_in[:, :], out_offset=bass.IndirectOffsetOnAxis(ap=pad_i[:, e:e + 1], axis=0),
                    in_=zero_rows, in_offset=None).then_inc(s_pad, 16)
            for r in range(RING):
                pool.wait_ge(s_ystore[r], MT // RING * 16)
            with pool.Fori(0, NT // TPB) as p:
                pool.wait_ge(s_gidx, p + 1)
                pool.sem_inc(s_held["pool"], 1)
                for r in range(TPB):
                    for k in range(2):
                        nc.gpsimd.indirect_dma_start(
                            out=gath[:, r, k, :], out_offset=None, in_=expert_out[:, :],
                            in_offset=bass.IndirectOffsetOnAxis(ap=gidx[:, r, k:k + 1], axis=0)).then_inc(s_gath[r], 16)

        @block.scalar
        def _(act):
            turn = Count()

            def take():
                act.wait_ge(s_turn, turn.next())
                return turnP[(turn.n - 1) % 2]

            def signal(to):
                act.wait_ge(s_turnread, turn.now())
                act.sem_inc(to, 1)

            act.wait_ge(s_bcol, 1)
            nc.scalar.activation(bcols[:].rearrange("p n c -> p (n c)"), outP[:, 0:3 * DC], ACT.Copy).then_inc(s_bcol, 1)
            act.wait_ge(s_setup_p, 1)
            nc.scalar.activation(WoT_sb, turnP[0][:].rearrange("p (c n) -> p c n", c=DC), ACT.Copy).then_inc(s_setup_c, 1)
            act.wait_ge(s_setup_p, 2)
            nc.scalar.activation(Aqk[:], turnP[1][:].rearrange("p (c n) -> p c n", c=DC), ACT.Copy).then_inc(s_setup_c, 1)
            act.wait_ge(s_setup_p, 3)
            nc.scalar.activation(a_bias[:], pvP[:, 0:DC], ACT.Copy, scale=SCALE).then_inc(s_setup_c, 1)
            nc.scalar.activation(w_rowc[:], pvP[:, 8:8 + DC], ACT.Copy).then_inc(s_setup_c, 1)
            nc.scalar.activation(rowc0[:], pvP[:, 16:17], ACT.Copy, scale=SCALE).then_inc(s_setup_c, 1)
            act.wait_ge(s_setup_p, 4)
            nc.scalar.activation(Cvo[:], turnP[0][:].rearrange("p (c n) -> p c n", c=DC), ACT.Copy).then_inc(s_setup_c, 1)
            act.wait_ge(s_setup_p, 5)
            nc.scalar.activation(out_bias[:], outP[:, 0:D], ACT.Copy).then_inc(s_setup_c, 1)

            def copy_memT(h, q):
                for g in GROUPS:
                    w = sum(rows(c) for c in g)
                    src = take()
                    nc.scalar.activation(memT[:, q, h, g[0] * P:g[0] * P + w], src[:, 0:w], ACT.Copy).then_inc(s_turnread, 1)

            def copy_xnT():
                for c in range(DC):
                    src = take()
                    nc.scalar.activation(xnT[:, c, :], src[:], ACT.Copy).then_inc(s_turnread, 1)

            def copy_qT(b, q):
                for c in range(DC):
                    src = take()
                    nc.scalar.activation(qT[:, c, :], src[:], ACT.Identity, scale=SCALE,
                                         bias=a_bias[:, c:c + 1]).then_inc(s_turnread, 1)
                src = take()
                nc.scalar.activation(rowc[:], src[:, 0:TPB], ACT.Identity, scale=SCALE, bias=rowc0[:, 0:1]).then_inc(s_turnread, 1)

            act.wait_ge(s_setup_c, SETUP_COPIES)
            for h in range(DC):
                copy_memT(h, 0)
            copy_xnT()
            copy_qT(0, 0)

            def step(t, b, j, par):
                if live(t, 0, NT):
                    if j == 0:
                        act.wait_ge(s_turnread, turn.now())
                    act.wait_ge(s_scored, t + 1)
                    if since(t, 2):
                        act.wait_ge(s_topk, t * TK - 2 * TK + 2)
                        act.wait_ge(s_exp, t * 2 - 2)
                    nc.scalar.activation(score[:, j % 2, :], scoreP[:, 0:S], ACT.Identity,
                                         bias=rowc[:, j:j + 1]).then_inc(s_score, 1)
                if live(t, 3, NT):
                    src = take()
                    if since(t, 4):
                        act.wait_ge(s_proj, t - 3)
                    nc.scalar.activation(attT[:], src[:, 0:D].rearrange("p (c n) -> p c n", c=DC), ACT.Copy).then_inc(s_turnread, 1)
                if live(t, 2, NT):
                    for g in GROUPS:
                        src = take()
                        if g[0] == 0 and since(t, 3):
                            act.wait_ge(s_pv, t - 2)
                        r = rows(g[-1])
                        nc.scalar.activation(probT[0:r, g[0]:g[-1] + 1, :],
                                             src[0:r, 0:len(g) * P].rearrange("p (c n) -> p c n", n=P),
                                             ACT.Copy).then_inc(s_turnread, 1)
                if j == 0 and live(b, 2, B):
                    for c in range(DC):
                        src = take()
                        nc.scalar.activation(xn2T[:, c, :], src[:], ACT.Copy).then_inc(s_turnread, 1)
                    src = take()
                    nc.scalar.activation(logit[:], src[:, 0:TPB * E].rearrange("p (j e) -> p j e", e=E),
                                         ACT.Copy).then_inc(s_turnread, 1)
                    signal(s_logit)
                if j == 1 and live(b, 2, B):
                    act.wait_ge(s_route, b * RK - 2 * RK + 2)
                    for n in range(TPB):
                        nc.scalar.activation(rexp[:, n, :], logit[:, n, :], ACT.Exp, bias=lneg[:, n:n + 1],
                                             accum_out=rexps[:, n:n + 1]).then_inc(s_rexp, 1)
                if j in (1, 2) and live(b, 2, B):
                    h = j - 1
                    src = take()
                    if h:
                        act.wait_ge(s_hid, b * 6 - 12 + 3)
                    elif since(b, 3):
                        act.wait_ge(s_shared, b - 2)
                    nc.scalar.activation(gateact[:, 0, :], src[:], ACT.Tanh, scale=0.5)
                    nc.scalar.activation(gateact[:, 1, :], src[:], ACT.Copy).then_inc(s_turnread, 1)
                    src = take()
                    nc.scalar.activation(gateact[:, 2, :], src[:], ACT.Copy, scale=0.5).then_inc(s_turnread, 1)
                    signal(s_sact)
                if j in (1, 2) and live(b, -1, B):
                    copy_memT(j - 1, (par + 1) % 2)
                if j == 2 and live(b, -1, B):
                    copy_xnT()
                if j == 3 and live(b, -1, B):
                    copy_qT(b + 1, (par + 1) % 2)
                if j == 3 and live(b, 2, B):
                    for n in range(0, TPB, 2):
                        src = take()
                        if n == 0:
                            act.wait_ge(s_hid, b * 6 - 6)
                        nc.scalar.activation(down[:, n:n + 2, :], src[:].rearrange("p (c n) -> p c n", c=2),
                                             ACT.Copy).then_inc(s_turnread, 1)
                    src = take()
                    nc.scalar.activation(rank[:], src[:, 0:TPB * E].rearrange("p (j e) -> p j e", e=E),
                                         ACT.Copy).then_inc(s_turnread, 1)
                    signal(s_rankc)
                if live(t, 2, NT):
                    act.wait_ge(s_pv, t - 1)
                    if since(t, 4):
                        act.wait_ge(s_proj, t - 3)
                        act.wait_ge(s_rsum, t - 3)
                    nc.scalar.activation(att[:, j % 2, :], pvP[:, 0:D + 1], ACT.Copy).then_inc(s_att, 1)
                if live(t, 1, NT):
                    q = (j - 1) % 2
                    act.wait_ge(s_neg, t)
                    nc.scalar.activation(prob, score[:, q, :], ACT.Exp, bias=negmax[:, q:q + 1]).then_inc(s_exp, 1)
                    act.wait_ge(s_topk, t * TK)
                    nc.scalar.activation(rest[:, q, :], rest[:, q, :], ACT.Exp, bias=negmax[:, q:q + 1]).then_inc(s_exp, 1)

            walk(act, step, turn)

            def estep(i, r):
                if live(i, 0, MT):
                    act.wait_ge(s_eturn, i + 1)
                    if since(i, 2):
                        act.wait_ge(s_gu, i - 1)
                    nc.scalar.activation(xinT[:, r % 2], turnP[r % 2][:, 0:D].rearrange("p (c n) -> p c n", c=DC),
                                         ACT.Copy).then_inc(s_eturnc, 1)
                if live(i, 1, MT):
                    act.wait_ge(s_gu, i)
                    if since(i, 3):
                        act.wait_ge(s_eh, i * 2 - 4)
                    q = (r - 1) % 2
                    nc.scalar.activation(etanh[:, q, :], guP[q][:, 0:F], ACT.Tanh, scale=0.5).then_inc(s_eact, 1)
                if live(i, 3, MT):
                    q = (r - 3) % RING
                    act.wait_ge(s_ydone, i - 2)
                    if since(i, RING // 2 + 3):
                        h = (q + RING // 2) % RING
                        act.wait_ge(s_ystore[h], (i - 3 - RING // 2 - h) * 2 + 16)
                    nc.scalar.activation(yout[:, q % (RING // 2), :], yP[q % 2][:, 0:D], ACT.Copy).then_inc(s_y, 1)
                if live(i, 4, MT):
                    q = (r - 4) % RING
                    act.wait_ge(s_y, i - 3)
                    act.dma_start(expert_out[bass.ds(i * P - 4 * P, P), :], yout[:, q % (RING // 2), :]).then_inc(s_ystore[q], 16)

            ewalk(act, estep)

        @block.vector
        def _(dve):
            def stats1(b):
                dve.wait_ge(s_x, b * 16 + 16)
                if since(b, 1):
                    dve.wait_ge(s_xn, b * TPB)
                dve.sem_inc(s_held["dve"], 1)
                for n in range(TPB):
                    nc.vector.bn_stats(stats[:, n, :], res[:, b * TPB + n, :]).then_inc(s_ln, 1)
                dve.wait_ge(s_ln, b * 8 + TPB)
                dve.sem_inc(s_held["dve"], 1)
                for n in range(TPB):
                    nc.vector.bn_aggr(meanvar[:, n, :], stats[:, n, :]).then_inc(s_ln, 1)

            def normed1(b):
                dve.wait_ge(s_lnp, b * 2 + 2)
                if since(b, 1):
                    dve.wait_ge(s_scored, b * TPB - TPB + 1)
                for n in range(TPB):
                    nc.vector.tensor_scalar(xn[:, n, :], res[:, b * TPB + n, :], meanvar[:, n, 0:1], rstd[:, n:n + 1],
                                            ALU.subtract, ALU.mult).then_inc(s_xn, 1)

            dve.wait_ge(s_const, 11)
            dve.wait_ge(s_bcol, 2)
            for c in range(DC):
                nc.vector.tensor_scalar(bq_wide[:, c, :], ones[:], bcols[:, 0, c:c + 1], None, ALU.mult).then_inc(s_wide, 1)
                nc.vector.tensor_scalar(bv_wide[:, c, :], ones[:], bcols[:, 2, c:c + 1], None, ALU.mult).then_inc(s_wide, 1)
            stats1(0)
            normed1(0)

            def step(t, b, j, par):
                if live(t, 4, NT):
                    q = j % 2
                    dve.wait_ge(s_att, t - 3)
                    if since(t, 6):
                        dve.wait_ge(s_res, t - 5)
                    nc.vector.reciprocal(rsum[:, q:q + 1], att[:, q, D:D + 1]).then_inc(s_rsum, 1)
                    dve.wait_ge(s_rsum, t - 3)
                    dve.wait_ge(s_proj, t - 3)
                    if j == 0:
                        dve.wait_ge(s_bias, b)
                    r = res[:, t - 4, :]
                    nc.vector.scalar_tensor_tensor(out=r, in0=outP[:, 0:D], scalar=rsum[:, q:q + 1], in1=r,
                                                   op0=ALU.mult, op1=ALU.add).then_inc(s_res, 1)
                    dve.wait_ge(s_res, t - 3)
                    dve.sem_inc(s_held["dve"], 1)
                    nc.vector.bn_stats(stats2[:, j, :], r).then_inc(s_ln2, 1)
                    dve.wait_ge(s_ln2, b * 8 - 8 + 2 * j + 1)
                if live(b, 2, B) and j == 0:
                    dve.wait_ge(s_ln2p, b * 2 - 2)
                    if since(b, 4):
                        dve.wait_ge(s_scat[par], (b - 2 - par) * (TPB * 16))
                    for n in range(TPB):
                        nc.vector.tensor_scalar(xn2[:, par, n, :], res[:, b * TPB - 2 * TPB + n, :],
                                                meanvar2[:, n, 0:1], rstd2[:, n:n + 1],
                                                ALU.subtract, ALU.mult).then_inc(s_xn2, 1)
                    dve.wait_ge(s_xn2, b * TPB - TPB)
                if live(t, 4, NT):
                    dve.sem_inc(s_held["dve"], 1)
                    nc.vector.bn_aggr(meanvar2[:, j, :], stats2[:, j, :]).then_inc(s_ln2, 1)
                if j == 0 and live(b, -1, B):
                    stats1(b + 1)
                if j == 1 and live(b, -1, B):
                    normed1(b + 1)
                r0 = b * RK - 2 * RK
                mt = bass.ds(b * TPB - 2 * TPB, TPB)
                if j == 1 and live(b, 2, B):
                    dve.wait_ge(s_logit, b - 1)
                    nc.vector.tensor_reduce(lneg[:], logit[:], AX_X, ALU.max).then_inc(s_route, 1)
                    dve.wait_ge(s_route, r0 + 1)
                    nc.vector.tensor_scalar(lneg[:], lneg[:], -1.0, None, ALU.mult).then_inc(s_route, 1)
                if j == 2 and live(b, 2, B):
                    dve.wait_ge(s_rexp, b * TPB - TPB)
                    nc.vector.reciprocal(rinv[:], rexps[:]).then_inc(s_route, 1)
                    dve.sem_inc(s_held["dve"], 1)
                    for n in range(TPB):
                        nc.vector.max(rtop[:, n, :], rexp[:, n, :]).then_inc(s_route, 1)
                    dve.wait_ge(s_route, r0 + 7)
                    dve.sem_inc(s_held["dve"], 1)
                    for n in range(TPB):
                        nc.vector.max_index(ridx[:, n, :], rtop[:, n, :], rexp[:, n, :]).then_inc(s_route, 1)
                    nc.vector.tensor_tensor(gates[:, mt, :], rtop[:, :, 0:2], rinv[:, :, None].to_broadcast([P, TPB, 2]),
                                            ALU.mult).then_inc(s_route, 1)
                    dve.wait_ge(s_route, r0 + 12)
                    nc.vector.tensor_copy(choice[:, mt, :], ridx[:, :, 0:2]).then_inc(s_route, 1)
                    dve.wait_ge(s_route, r0 + 13)
                    nc.vector.tensor_tensor(onehot[:], iotaE[:, None, None, :].to_broadcast([P, TPB, 2, E]),
                                            choice[:, mt, :, None].to_broadcast([P, TPB, 2, E]), ALU.is_equal).then_inc(s_route, 1)
                    dve.wait_ge(s_route, r0 + 14)
                    if since(b, 3):
                        dve.wait_ge(s_rankc, b - 2)
                    nc.vector.tensor_tensor(chosen[:], onehot[:, :, 0, :], onehot[:, :, 1, :], ALU.add).then_inc(s_route, 1)

                if live(t, 0, NT):
                    q, k0 = j % 2, t * TK
                    dve.wait_ge(s_score, t + 1)
                    if since(t, 2):
                        dve.wait_ge(s_exp, t * 2 - 2)
                        dve.wait_ge(s_masked, t - 1)
                    dve.sem_inc(s_held["dve"], 1)
                    nc.vector.max(best[:, q, 0:8], score[:, q, :]).then_inc(s_topk, 1)
                    dve.wait_ge(s_topk, k0 + 1)
                    nc.vector.tensor_scalar(negmax[:, q:q + 1], best[:, q, 0:1], -1.0, None, ALU.mult).then_inc(s_neg, 1)
                    nc.vector.match_replace(rest[:, q, :], best[:, q, 0:8], score[:, q, :], GONE).then_inc(s_topk, 1)
                    for n in range(1, ROUNDS):
                        b8 = best[:, q, 8 * n:8 * n + 8]
                        dve.wait_ge(s_topk, k0 + 2 * n)
                        dve.sem_inc(s_held["dve"], 1)
                        nc.vector.max(b8, rest[:, q, :]).then_inc(s_topk, 1)
                        dve.wait_ge(s_topk, k0 + 2 * n + 1)
                        dve.sem_inc(s_held["dve"], 1)
                        nc.vector.match_replace(rest[:, q, :], b8, rest[:, q, :], GONE).then_inc(s_topk, 1)

                if j == 3 and live(b, 2, B):
                    dve.wait_ge(s_rankc, b - 1)
                    nc.vector.tensor_tensor(rank[:], rank[:], ebase[:, None, :].to_broadcast([P, TPB, E]), ALU.add).then_inc(s_route, 1)
                    dve.wait_ge(s_route, r0 + 16)
                    nc.vector.tensor_tensor(onehot[:], onehot[:], rank[:, :, None, :].to_broadcast([P, TPB, 2, E]),
                                            ALU.mult).then_inc(s_route, 1)
                    dve.wait_ge(s_route, r0 + 17)
                    nc.vector.tensor_reduce(slot[:, mt, :], onehot[:], AX_X, ALU.add).then_inc(s_route, 1)
                    dve.wait_ge(s_route, r0 + 18)
                    if since(b, 4):
                        dve.wait_ge(s_scat[par], (b - 2 - par) * (TPB * 16))
                    dve.sem_inc(s_held["dve"], 1)
                    nc.vector.tensor_copy(slot_i[:, par, :, :], slot[:, mt, :]).then_inc(s_route, 1)

            walk(dve, step)

            done = Count()

            def then(ins):
                ins.then_inc(s_plan, 1)
                dve.wait_ge(s_plan, done.next())

            dve.wait_ge(s_count, 1)
            dve.wait_ge(s_iota, 1)
            nc.vector.memset(zero_rows, 0.0).then_inc(s_zero, 1)
            then(nc.vector.tensor_copy(count, turnP[0][:, 0:E]))
            then(nc.vector.tensor_scalar(tiles_i[:], count, 1.0 / P, (P - 1.0) / P - 0.5 + 0.5 / P, ALU.mult, ALU.add))
            then(nc.vector.tensor_copy(tiles, tiles_i[:]))
            then(nc.vector.tensor_copy(incl[0], tiles))
            n, a = 1, 0
            while n < E:
                then(nc.vector.tensor_copy(incl[1 - a][:, 0:n], incl[a][:, 0:n]))
                then(nc.vector.tensor_tensor(incl[1 - a][:, n:E], incl[a][:, n:E], incl[a][:, 0:E - n], ALU.add))
                n, a = 2 * n, 1 - a
            upto = incl[a]
            then(nc.vector.tensor_tensor(excl, upto, tiles, ALU.subtract))
            then(nc.vector.scalar_tensor_tensor(out=shift, in0=excl, scalar=float(P), in1=ebase[:], op0=ALU.mult, op1=ALU.subtract))
            then(nc.vector.tensor_tensor(shifted, iotaE[:, None, :].to_broadcast([P, 2 * NT, E]),
                                         choice[:].rearrange("p t k -> p (t k)")[:, :, None].to_broadcast([P, 2 * NT, E]),
                                         ALU.is_equal))
            then(nc.vector.tensor_tensor(shifted, shifted, shift[:, None, :].to_broadcast([P, 2 * NT, E]), ALU.mult))
            then(nc.vector.tensor_reduce(yrow, shifted, AX_X, ALU.add))
            then(nc.vector.tensor_tensor(yrow_i.rearrange("p t k -> p (t k)"), yrow,
                                         slot[:].rearrange("p t k -> p (t k)"), ALU.add))
            then(nc.vector.tensor_scalar(lastt, upto[:, E - 1:E], -1.0, None, ALU.add))
            then(nc.vector.tensor_scalar(tidx, iota_t, lastt, None, ALU.min))
            then(nc.vector.tensor_tensor(passed, tidx[:, :, None].to_broadcast([P, MT, E]),
                                         upto[:, None, :].to_broadcast([P, MT, E]), ALU.is_ge))
            then(nc.vector.tensor_reduce(trow, passed, AX_X, ALU.add))
            then(nc.vector.tensor_copy(tile_expert, trow))
            then(nc.vector.tensor_scalar(gap, tiles, -float(P), float(EROWS), ALU.mult, ALU.add))
            then(nc.vector.tensor_tensor(passed, passed, gap[:, None, :].to_broadcast([P, MT, E]), ALU.mult))
            then(nc.vector.tensor_reduce(trow, passed, AX_X, ALU.add))
            then(nc.vector.scalar_tensor_tensor(out=tile_row, in0=tidx, scalar=float(P), in1=trow, op0=ALU.mult, op1=ALU.add))
            then(nc.vector.tensor_tensor(padf, count, ebase[:], ALU.add))
            then(nc.vector.tensor_scalar(pad_i[:], padf, iota_p[:, 0:1], None, ALU.add))
            assert done.n == PLAN

            def estep(i, r):
                if live(i, 1, MT):
                    q = (r - 1) % 2
                    g, u = guP[q][:, 0:F], guP[q][:, F:2 * F]
                    dve.wait_ge(s_eact, i)
                    if since(i, 3):
                        dve.wait_ge(s_ehT, i - 2)
                    nc.vector.scalar_tensor_tensor(out=ehid[:, q, :], in0=etanh[:, q, :], scalar=1.0, in1=g,
                                                   op0=ALU.add, op1=ALU.mult).then_inc(s_eh, 1)
                    dve.wait_ge(s_eh, i * 2 - 1)
                    nc.vector.scalar_tensor_tensor(out=ehid[:, q, :], in0=ehid[:, q, :], scalar=0.5, in1=u,
                                                   op0=ALU.mult, op1=ALU.mult).then_inc(s_eh, 1)
                if live(i, 2, MT):
                    q = r % 2
                    dve.wait_ge(s_ehT, i - 1)
                    if since(i, 4):
                        dve.wait_ge(s_ydone, i - 3)
                    nc.vector.tensor_copy(ehidT[:, q, :], ehTP[q][:, 0:P]).then_inc(s_ehTc, 1)

            ewalk(dve, estep)

            dve.wait_ge(s_shared, B)
            with dve.Fori(0, NT // TPB) as p:
                for r in range(TPB):
                    dve.wait_ge(s_gath[r], p * 32)
                dve.sem_inc(s_held["dve"], 1)
                nc.vector.tensor_copy(gidx[:], yrow_i[:, bass.ds(p * TPB, TPB), :]).then_inc(s_gidx, 1)
                for r in range(TPB):
                    tile = p * TPB + r
                    rr = res[:, tile, :]
                    dve.wait_ge(s_gath[r], p * 32 + 32)
                    for k in range(2):
                        if k:
                            dve.wait_ge(s_final, p * (2 * TPB) + 2 * r + 1)
                        nc.vector.scalar_tensor_tensor(out=rr, in0=gath[:, r, k, :], scalar=gates[:, tile, k:k + 1], in1=rr,
                                                       op0=ALU.mult, op1=ALU.add).then_inc(s_final, 1)

        @block.tensor
        def _(pe):
            pe.wait_ge(s_const, 11)
            pe.wait_ge(s_small, 16 * 8)
            pe.transpose(outP[:, 0:3 * DC], brows, ident[0:3 * DC, 0:3 * DC]).then_inc(s_bcol, 1)
            for oc in range(DC):
                for c in range(DC):
                    mm = pe.transpose(turnP[0][:, oc * D + c * P:oc * D + (c + 1) * P], Wo_sb[:, c, oc * P:(oc + 1) * P], ident[:])
            mm.then_inc(s_setup_p, 1)

            def product(to, terms):
                for n, (lhsT, rhs) in enumerate(terms):
                    mm = pe.matmul(to, lhsT, rhs, start=(n == 0), stop=(n == len(terms) - 1))
                return mm

            for c in range(DC):
                mm = product(turnP[1][:, c * D:(c + 1) * D], [(Wq_sb[:, o, c * P:(c + 1) * P], Wk_sb[:, o, :]) for o in range(DC)])
            mm.then_inc(s_setup_p, 1)
            pe.wait_ge(s_bcol, 2)
            pe.wait_ge(s_wide, 2 * DC)
            for c in range(DC):
                product(pvP[:, c:c + 1], [(Wk_sb[:, o, c * P:(c + 1) * P], bcols[:, 0, o:o + 1]) for o in range(DC)])
                product(pvP[:, 8 + c:9 + c], [(Wq_sb[:, o, c * P:(c + 1) * P], bcols[:, 1, o:o + 1]) for o in range(DC)])
            product(pvP[:, 16:17], [(bq_wide[:, o, :], bcols[:, 1, o:o + 1]) for o in range(DC)]).then_inc(s_setup_p, 1)
            pe.wait_ge(s_setup_c, 1)
            for c in range(DC):
                mm = product(turnP[0][:, c * D:(c + 1) * D], [(Wv_sb[:, o, c * P:(c + 1) * P], WoT_sb[:, o, :]) for o in range(DC)])
            mm.then_inc(s_setup_p, 1)
            product(outP[:, 0:D], [(bv_wide[:, o, :], WoT_sb[:, o, :]) for o in range(DC)]
                    + [(ones[0:1, :], bo_row[0:1, :])]).then_inc(s_setup_p, 1)
            pe.wait_ge(s_setup_c, SETUP_COPIES)

            turn = Count()

            def give():
                n = turn.next()
                if not isinstance(n, int) or n > 2:
                    pe.wait_ge(s_turnread, turn.now(2))
                return turnP[(turn.n - 1) % 2]

            def turn_mem(b, h, q):
                if h == 0:
                    pe.wait_ge(s_mem[q], (b - q) * 16 + 32)
                for g in GROUPS:
                    to = give()
                    for n, c in enumerate(g):
                        mm = pe.transpose(to[:, n * P:n * P + rows(c)], mem[0:rows(c), q, c, h * P:(h + 1) * P],
                                          ident[0:rows(c), 0:rows(c)])
                    mm.then_inc(s_turn, 1)

            def turn_xn(src, ready, n0):
                pe.wait_ge(ready, n0)
                for c in range(DC):
                    to = give()
                    for n in range(TPB):
                        mm = pe.transpose(to[:, n * P:(n + 1) * P], src(n, c), ident[:])
                    mm.then_inc(s_turn, 1)

            def query(b):
                pe.wait_ge(s_turnread, turn.now())
                for c in range(DC):
                    product(give()[:], [(Aqk[:, k, c * P:(c + 1) * P], xnT[:, k, :]) for k in range(DC)]).then_inc(s_turn, 1)
                to = give()
                for n in range(TPB):
                    mm = product(to[:, n:n + 1], [(xnT[:, k, n * P:(n + 1) * P], w_rowc[:, k:k + 1]) for k in range(DC)])
                mm.then_inc(s_turn, 1)

            def xn_part(n, c):
                return xn[:, n, c * P:(c + 1) * P]

            for h in range(DC):
                turn_mem(0, h, 0)
            turn_xn(xn_part, s_xn, TPB)
            query(0)

            def step(t, b, j, par):
                if live(t, 0, NT):
                    if j == 0:
                        pe.wait_ge(s_turnread, turn.now())
                    if since(t, 1):
                        pe.wait_ge(s_score, t)
                    for a, z in CHUNKS:
                        mm = product(scoreP[:, a:z], [(qT[:, k, j * P:(j + 1) * P], memT[:, par, k, a:z]) for k in range(DC)])
                    mm.then_inc(s_scored, 1)
                if live(t, 3, NT):
                    pe.wait_ge(s_att, t - 2)
                    to = give()
                    attT_copied = turn.now()
                    for c in range(DC):
                        mm = pe.transpose(to[:, c * P:(c + 1) * P], att[:, (j - 3) % 2, c * P:(c + 1) * P], ident[:])
                    mm.then_inc(s_turn, 1)
                if live(t, 2, NT):
                    q, mq = j % 2, par if j >= 2 else (par + 1) % 2
                    pe.wait_ge(s_masked, t - 1)
                    for g in GROUPS:
                        to = give()
                        for n, c in enumerate(g):
                            mm = pe.transpose(to[0:rows(c), n * P:(n + 1) * P], prob[:, c * P:c * P + rows(c)], ident[:])
                        mm.then_inc(s_turn, 1)
                    pe.wait_ge(s_turnread, turn.now())
                    if since(t, 3):
                        pe.wait_ge(s_att, t - 2)
                    product(pvP[:, 0:D + 1], [(probT[0:rows(c), c, :], mem[0:rows(c), mq, c, :]) for c in range(SC)]).then_inc(s_pv, 1)
                if live(t, 3, NT):
                    pe.wait_ge(s_turnread, attT_copied)
                    if since(t, 4):
                        pe.wait_ge(s_res, t - 3)
                    product(outP[:, 0:D], [(attT[:, k, :], Cvo[:, k, :]) for k in range(DC)]).then_inc(s_proj, 1)
                if j == 0 and live(b, 2, B):
                    turn_xn(lambda n, c: xn2[:, par, n, c * P:(c + 1) * P], s_xn2, b * TPB - TPB)
                    pe.wait_ge(s_turnread, turn.now())
                    if isinstance(b, int) and b == 2 or not isinstance(b, int):
                        pe.wait_ge(s_weights, NWEIGHTS)
                    to = give()
                    for n in range(TPB):
                        mm = product(to[:, n * E:(n + 1) * E], [(xn2T[:, k, n * P:(n + 1) * P], Wr_sb[:, k, :]) for k in range(DC)])
                    mm.then_inc(s_turn, 1)
                if j in (1, 2) and live(b, 2, B):
                    for w in range(2):
                        f = w * FS + (j - 1) * P
                        product(give()[:], [(Sgu_sb[:, k, f:f + P], xn2T[:, k, :]) for k in range(DC)]).then_inc(s_turn, 1)
                if j in (1, 2) and live(b, -1, B):
                    turn_mem(b + 1, j - 1, (par + 1) % 2)
                if j == 2 and live(b, -1, B):
                    turn_xn(xn_part, s_xn, b * TPB + 2 * TPB)
                if j == 3 and live(b, -1, B):
                    query(b + 1)
                if j == 3 and live(b, 2, B):
                    pe.wait_ge(s_hid, b * 6 - 6)
                    for n in range(0, TPB, 2):
                        to = give()
                        for m in range(2):
                            mm = product(to[:, m * D:(m + 1) * D],
                                         [(hid[:, f, (n + m) * P:(n + m + 1) * P], Sd_sb[:, f, :]) for f in range(FC)])
                        mm.then_inc(s_turn, 1)
                    pe.wait_ge(s_route, b * RK - 2 * RK + 15)
                    pe.wait_ge(s_cum, b * 5 - 10 + TPB)
                    product(give()[:, 0:TPB * E],
                            [(before[:], chosen[:].rearrange("p j e -> p (j e)")),
                             (ones[:], cum[:, 0:TPB, :].rearrange("p j e -> p (j e)"))]).then_inc(s_turn, 1)

            walk(pe, step, turn)

            pe.wait_ge(s_cum, 5 * B)
            pe.wait_ge(s_turnread, turn.now())
            product(turnP[0][:, 0:E], [(ones[:], cum[:, 0, :])]).then_inc(s_count, 1)
            pe.wait_ge(s_plan, PLAN)
            pe.wait_ge(s_res, NT)
            pe.wait_ge(s_late, 144)

            def estep(i, r):
                if live(i, 0, MT):
                    pe.wait_ge(s_ein[r], (i - r) * 2 + 16)
                    if since(i, 2):
                        pe.wait_ge(s_eturnc, i - 1)
                    for c in range(DC):
                        mm = pe.transpose(turnP[r % 2][:, c * P:(c + 1) * P], xin[:, r, c * P:(c + 1) * P], ident[:])
                    mm.then_inc(s_eturn, 1)
                if live(i, 2, MT):
                    q = r % 2
                    pe.wait_ge(s_eh, i * 2 - 2)
                    if since(i, 4):
                        pe.wait_ge(s_ehTc, i - 3)
                    pe.transpose(ehTP[q][:, 0:P], ehid[:, q, :], ident[:]).then_inc(s_ehT, 1)
                if live(i, 1, MT):
                    q = (r - 1) % 2
                    e = pe.value_load(tile_expert[0:1, bass.ds(i - 1, 1)], min_val=0, max_val=E - 1)
                    pe.wait_ge(s_eturnc, i)
                    if since(i, 3):
                        pe.wait_ge(s_eh, i * 2 - 4)
                    product(guP[q][:, 0:2 * F], [(xinT[:, q, k, :], Wgu_sb[k][:, bass.ds(e, 1), :]) for k in range(DC)]).then_inc(s_gu, 1)
                if live(i, 3, MT):
                    q = (r - 3) % 2
                    e = pe.value_load(tile_expert[0:1, bass.ds(i - 3, 1)], min_val=0, max_val=E - 1)
                    pe.wait_ge(s_ehTc, i - 2)
                    if since(i, 5):
                        pe.wait_ge(s_y, i - 4)
                    product(yP[q][:, 0:D], [(ehidT[:, q, :], Wd_sb[:, bass.ds(e, 1), :])]).then_inc(s_ydone, 1)

            ewalk(pe, estep)


_INS = ["x", "ctx_1024", "L0_xattn_Wq", "L0_xattn_bq", "L0_xattn_Wk", "L0_xattn_bk", "L0_xattn_Wv", "L0_xattn_bv",
        "L0_xattn_Wo", "L0_xattn_bo", "L0_ffn_Wr", "L0_ffn_Wg", "L0_ffn_Wu", "L0_ffn_Wd", "L0_ffn_Sg", "L0_ffn_Su", "L0_ffn_Sd"]


def kernel(**inputs):
    import numpy as _np
    import concourse.bacc as _bacc
    from concourse import mybir as _mybir
    from concourse.bass_utils import run_bass_kernel_spmd as _run

    nc = _bacc.Bacc("TRN2", target_bir_lowering=False, num_devices=1)
    arrays, args = {}, []
    for name in _INS:
        a = _np.ascontiguousarray(inputs[name])
        arrays[f"in_{name}_dram"] = a
        args.append(nc.dram_tensor(f"in_{name}_dram", a.shape, _mybir.dt.from_np(a.dtype), kind="ExternalInput").ap())
    shape = _np.shape(inputs["x"])
    args.append(nc.dram_tensor("out_0_dram", shape, _mybir.dt.float32, kind="ExternalOutput").ap())
    xattn_moe_kernel(nc, *args)
    r = _run(nc, [arrays], core_ids=[0])
    return r.results[0]["out_0_dram"]
```

```python
from contextlib import ExitStack

import concourse.bass as bass
from concourse import mybir

P = 128
F32 = mybir.dt.float32
BF16 = mybir.dt.bfloat16
I32 = mybir.dt.int32
U32 = mybir.dt.uint32
ALU = mybir.AluOpType
ACT = mybir.ActivationFunctionType
AX_X = mybir.AxisListType.X

TOP_K = 32
ROUNDS = TOP_K // 8
LN_EPS = 1e-5
GONE = -3.0e38
TPB = 4


class Count:

    def __init__(self):
        self.base, self.n = 0, 0

    def next(self):
        self.n += 1
        return self.now()

    def now(self, back=0):
        return self.base + (self.n - back)

    def at(self, base):
        self.base, self.n = base, 0


def since(v, first):
    return not isinstance(v, int) or v >= first


def live(v, lag, n):
    return not isinstance(v, int) or 0 <= v - lag < n


def xattn_moe_kernel(nc, x, ctx_1024, Wq, bq, Wk, bk, Wv, bv, Wo, bo, Wr, Wg, Wu, Wd, Sg, Su, Sd, out):
    B, T, D = x.shape
    S = ctx_1024.shape[1]
    E, _, F = Wg.shape
    FS = Sg.shape[1]
    DC = D // P
    FC = FS // P
    NT = B * T // P
    SF = S // P
    SR = S - SF * P
    SC = SF + 1
    SCALE = float(D) ** -0.5
    assert T == TPB * P and D == 2 * P and F == P and FS == 2 * P and B % 2 == 0 and B >= 6 and 0 < SR < P
    EROWS = B * T + P
    MT = 2 * NT + E
    RING = 8
    TURN = 2 * RING
    assert MT % TURN == 0
    GROUPS = [list(range(g, min(g + 4, SC))) for g in range(0, SC, 4)]
    NG = len(GROUPS)
    CHUNKS = [(c, min(c + 512, S)) for c in range(0, S, 512)]
    TK = 2 * ROUNDS
    RK = 19
    PREP_TURNS = DC * NG + 2 * DC + 1
    BATCH_TURNS = TPB * (NG + 1) + PREP_TURNS + DC + 1 + 2 * FC + TPB // 2 + 1

    def rows(c):
        return P if c < SF else SR

    x_t = x.rearrange("b (j p) d -> p (b j) d", p=P)
    out_t = out.rearrange("b (j p) d -> p (b j) d", p=P)

    with ExitStack() as ctx:
        def sb(name, shape, dt=F32):
            return ctx.enter_context(nc.sbuf_tensor(name, shape, dt))

        def psum(name, shape, dt=F32):
            return ctx.enter_context(nc.psum_tensor(name, shape, dt))

        def sem(name):
            return ctx.enter_context(nc.semaphore(name))

        expert_in = nc.dram_tensor("expert_in", [E * EROWS, D], F32, kind="Internal").ap()
        expert_out = nc.dram_tensor("expert_out", [MT * P, D], F32, kind="Internal").ap()

        res = sb("res", [P, NT, D])
        mem = sb("mem", [P, 2, SC, D + 1])
        memT = sb("memT", [P, 2, DC, S])
        work = sb("work", [P, 5, S])
        score, rest, prob = work[:, 0:2, :], work[:, 2:4, :], work[:, 4, :]
        probT = sb("probT", [P, SC, P])
        qT = sb("qT", [P, DC, T])
        xnT = sb("xnT", [P, DC, T])
        xn = sb("xn", [P, TPB, D])
        xn2 = sb("xn2", [P, 2, TPB, D])
        xn2T = sb("xn2T", [P, DC, T])
        gateact = sb("gateact", [P, 3, T])
        hid = sb("hid", [P, FC, T])
        down = gateact[:, 0:2, :].rearrange("p c (h d) -> p (c h) d", h=2)
        att = sb("att", [P, 2, D + 1])
        attT = sb("attT", [P, DC, P])
        best = sb("best", [P, 2, 8 * ROUNDS])
        negmax = sb("negmax", [P, 2])
        rowc = sb("rowc", [P, TPB])
        rsum = sb("rsum", [P, 2])
        stats = sb("stats", [P, TPB, 6])
        meanvar = sb("meanvar", [P, TPB, 2])
        rstd = sb("rstd", [P, TPB])
        stats2 = sb("stats2", [P, TPB, 6])
        meanvar2 = sb("meanvar2", [P, TPB, 2])
        rstd2 = sb("rstd2", [P, TPB])
        eps = sb("eps", [P, TPB])
        minus_half = sb("minus_half", [P, TPB])
        ident = sb("ident", [P, P])
        before = sb("before", [P, P])
        ones = sb("ones", [P, P])
        iotaE = sb("iotaE", [P, E])
        ebase = sb("ebase", [P, E])
        Sgu_sb = sb("Sgu_sb", [P, DC, 2 * FS])
        Sd_sb = sb("Sd_sb", [P, FC, D])
        Wr_sb = sb("Wr_sb", [P, DC, E])
        Aqk = sb("Aqk", [P, DC, D])
        Cvo = sb("Cvo", [P, DC, D])
        bcols = sb("bcols", [P, 3, DC])
        a_bias = sb("a_bias", [P, DC])
        w_rowc = sb("w_rowc", [P, DC])
        rowc0 = sb("rowc0", [P, 1])
        out_bias = sb("out_bias", [P, D])
        logit = sb("logit", [P, TPB, E])
        lneg = sb("lneg", [P, TPB])
        rexp = sb("rexp", [P, TPB, E])
        rexps = sb("rexps", [P, TPB])
        rinv = sb("rinv", [P, TPB])
        rtop = sb("rtop", [P, TPB, 8])
        ridx = sb("ridx", [P, TPB, 8], U32)
        chosen = sb("chosen", [P, TPB, E])
        cum = sb("cum", [P, TPB + 1, E])
        rank = sb("rank", [P, TPB, E])
        onehot = sb("onehot", [P, TPB, 2, E])
        choice = sb("choice", [P, NT, 2])
        slot = sb("slot", [P, NT, 2])
        gates = sb("gates", [P, NT, 2])
        slot_i = sb("slot_i", [P, 2, TPB, 2], I32)
        tiles_i = sb("tiles_i", [P, E], I32)
        gidx = sb("gidx", [P, 2, TPB, 2], I32)
        pad_row = sb("pad_row", [P, E], I32)

        def weight(buf, i, w):
            return buf[:, i, w * DC * D:(w + 1) * DC * D].rearrange("p (c n) -> p c n", c=DC)

        Wq_sb, Wk_sb, Wv_sb, Wo_sb = weight(work, 2, 0), weight(work, 2, 1), weight(work, 2, 2), weight(work, 3, 0)
        WoT_sb = weight(work, 4, 0)
        brows, bo_row = work[0:3 * DC, 0, 0:P], work[0:1, 1, 0:D]
        bq_wide, bv_wide = (work[:, 4, (2 + i) * DC * P + D:(3 + i) * DC * P + D].rearrange("p (c n) -> p c n", c=DC)
                            for i in range(2))

        scoreP = psum("scoreP", [P, 2048])
        turnP = [psum(f"turnP{i}", [P, 512]) for i in range(2)]
        pvP = psum("pvP", [P, 512])
        outP = psum("outP", [P, 512])

        SETUP_COPIES = 7
        NWEIGHTS = 16 * 4
        PADS_PLANNED = 3
        TILES_PLANNED = PADS_PLANNED + 3 + 2 * 4 + 9
        PLAN = TILES_PLANNED + 6

        flat_mem, flat_memT, flat_work = (mem[:].rearrange("p a c d -> p (a c d)"), memT[:].rearrange("p a c s -> p (a c s)"),
                                          work[:].rearrange("p a s -> p (a s)"))
        at = [0]

        def reuse(of, n):
            at[0] += n
            assert at[0] <= of.shape[1]
            return of[:, at[0] - n:at[0]]

        Wgu1_sb = reuse(flat_mem, E * 2 * F).rearrange("p (e f) -> p e f", e=E)
        xin = reuse(flat_mem, RING * D).rearrange("p (r d) -> p r d", r=RING)
        zero_rows = reuse(flat_mem, D)
        at[0] = 0
        Wd_sb = reuse(flat_memT, E * D).rearrange("p (e d) -> p e d", e=E)
        passed = reuse(flat_memT, MT * E).rearrange("p (t e) -> p t e", e=E)
        at[0] = 0
        Wgu0_sb = reuse(flat_work, E * 2 * F).rearrange("p (e f) -> p e f", e=E)
        shifted = reuse(flat_work, 2 * NT * E).rearrange("p (t e) -> p t e", e=E)
        count, tiles, incl0, incl1, excl, shift, gap, padf = (reuse(flat_work, E) for _ in range(8))
        lastt, yrow, tidx, trow = (reuse(flat_work, n) for n in (1, 2 * NT, MT, MT))
        at[0] = 0
        gath = reuse(flat_work, 2 * TPB * 2 * D).rearrange("p (r k d) -> p r k d", r=2 * TPB, k=2)
        at[0] = E * 2 * F
        yout = reuse(flat_work, RING // 2 * D).rearrange("p (r d) -> p r d", r=RING // 2)
        incl = [incl0, incl1]
        Wgu_sb = [Wgu0_sb, Wgu1_sb]
        xinT = qT[:].rearrange("p c t -> p (c t)")[:, 0:2 * D].rearrange("p (q c n) -> p q c n", q=2, c=DC)
        etanh, ehid, ehidT = (xnT[:, 0, 0:2 * P].rearrange("p (q n) -> p q n", q=2),
                              xnT[:, 0, 2 * P:4 * P].rearrange("p (q n) -> p q n", q=2),
                              xnT[:, 1, 0:2 * P].rearrange("p (q n) -> p q n", q=2))
        flat_probT = probT[:].rearrange("p c n -> p (c n)")
        at[0] = 0
        iota_t = reuse(flat_probT, MT)
        yrow_i = reuse(flat_probT, 2 * NT).bitcast(I32).rearrange("p (t k) -> p t k", k=2)
        tile_row, tile_expert = (reuse(flat_probT, MT).bitcast(I32) for _ in range(2))
        guP = [scoreP[:, 512 * i:512 * i + 512] for i in range(2)]
        ehTP = [scoreP[:, 512 * i:512 * i + 512] for i in range(2, 4)]
        yP = [pvP, outP]

        s_small = sem("small_loaded")
        s_weights = sem("ffn_weights_loaded")
        s_x = sem("x_loaded")
        s_late = sem("late_weights_loaded")
        s_mem = [sem(f"mem_loaded{i}") for i in range(2)]
        s_const = sem("constants_made")
        s_wide = sem("wide_biases")
        s_bcol = sem("bias_columns")
        s_setup_p = sem("setup_product")
        s_setup_c = sem("setup_copied")
        s_scored = sem("scores_in_psum")
        s_score = sem("scores_copied")
        s_topk = sem("topk_step")
        s_neg = sem("negmax_ready")
        s_exp = sem("exps_done")
        s_masked = sem("prob_masked")
        s_turn = sem("turned")
        s_turnread = sem("turn_read")
        s_pv = sem("pv_done")
        s_att = sem("att_copied")
        s_proj = sem("proj_done")
        s_rsum = sem("rsum_ready")
        s_res = sem("residual_added")
        s_ln = sem("ln1_stats")
        s_lnp = sem("ln1_rstd")
        s_xn = sem("xn_ready")
        s_bias = sem("bias_added")
        s_ln2 = sem("ln2_stats")
        s_ln2p = sem("ln2_rstd")
        s_xn2 = sem("xn2_ready")
        s_logit = sem("logits_copied")
        s_rankc = sem("ranks_copied")
        s_route = sem("route_step")
        s_rexp = sem("route_exp")
        s_cum = sem("cum_step")
        s_scat = [sem(f"rows_scattered{i}") for i in range(2)]
        s_sact = sem("shared_act")
        s_hid = sem("hidden_step")
        s_down = sem("shared_down_copied")
        s_shared = sem("shared_added")
        s_held = {k: sem(f"held_{k}") for k in ("pool", "dve")}
        s_count = sem("counts_summed")
        s_plan = sem("plan_step")
        s_iota = sem("tile_numbers_made")
        s_zero = sem("zero_rows_made")
        s_pad = sem("pad_rows_written")
        s_ein = [sem(f"expert_rows_loaded{i}") for i in range(RING)]
        s_eturn = sem("expert_rows_turned")
        s_eturnc = sem("expert_rows_copied")
        s_gu = sem("gate_up_done")
        s_eact = sem("expert_tanh")
        s_eh = sem("expert_hidden_step")
        s_ehT = sem("expert_hidden_turned")
        s_ehTc = sem("expert_hiddenT_copied")
        s_ydone = sem("expert_out_product")
        s_y = sem("expert_out_copied")
        s_ystore = [sem(f"expert_out_stored{i}") for i in range(RING)]
        s_gidx = sem("gather_rows_ready")
        s_gath = [sem(f"rows_gathered{i}") for i in range(2 * TPB)]
        s_final = sem("final_step")
        s_out = sem("out_stored")

        block = ctx.enter_context(nc.Block())

        PAIR = 2 * TPB
        NP = B // 2

        def walk(eng, step, turn=None):
            for t in range(PAIR):
                step(t, t // TPB, t % TPB, t // TPB % 2)
            if turn:
                first, per = turn.n, 2 * BATCH_TURNS
                assert first % 2 == 0 and per % 2 == 0
            with eng.Fori(1, NP - 1) as p:
                if turn:
                    turn.at(p * per + (first - per))
                for j in range(PAIR):
                    step(p * PAIR + j, p * 2 + j // TPB, j % TPB, j // TPB)
                assert turn is None or turn.n == per
            if turn:
                turn.at((NP - 2) * per + first)
            for t in range(NT - PAIR, NT + 2 * TPB):
                step(t, t // TPB, t % TPB, t // TPB % 2)

        def ewalk(eng, step):
            for i in range(TURN):
                step(i, i)
            with eng.Fori(1, MT // TURN) as p:
                for r in range(TURN):
                    step(p * TURN + r, r)
            for i in range(MT, MT + 6):
                step(i, i % TURN)

        @block.sync
        def _(sp):
            def load_x(b):
                sp.dma_start(res[:, bass.ds(b * TPB, TPB), :], x_t[:, bass.ds(b * TPB, TPB), :]).then_inc(s_x, 16)

            def load_mem(b, par):
                src = ctx_1024[bass.ds(b, 1), :, :]
                sp.dma_start(mem[:, par, 0:SF, 0:D],
                             src[:, 0:SF * P, :].rearrange("a (c p) d -> p (a c) d", p=P)).then_inc(s_mem[par], 16)
                sp.dma_start(mem[0:SR, par, SF, 0:D],
                             src[:, SF * P:S, :].rearrange("a p d -> p (a d)")).then_inc(s_mem[par], 16)

            load_x(0)
            for w_sb, w in ((Wq_sb, Wq), (Wk_sb, Wk), (Wv_sb, Wv), (Wo_sb, Wo)):
                sp.dma_start(w_sb, w.rearrange("(c p) n -> p c n", p=P)).then_inc(s_small, 16)
            for n, bias in enumerate((bq, bk, bv)):
                sp.dma_start(brows[n * DC:(n + 1) * DC, :], bias.rearrange("(c p) -> c p", p=P)).then_inc(s_small, 16)
            sp.dma_start(bo_row[:, :], bo.rearrange("(a n) -> a n", a=1)).then_inc(s_small, 16)
            load_mem(0, 0)
            sp.wait_ge(s_x, 16)
            load_x(1)
            load_mem(1, 1)
            sp.dma_start(Wr_sb[:], Wr.rearrange("(c p) e -> p c e", p=P)).then_inc(s_weights, 16)
            sp.dma_start(Sgu_sb[:, :, 0:FS], Sg.rearrange("(c p) f -> p c f", p=P)).then_inc(s_weights, 16)
            sp.dma_start(Sgu_sb[:, :, FS:2 * FS], Su.rearrange("(c p) f -> p c f", p=P)).then_inc(s_weights, 16)
            sp.dma_start(Sd_sb[:], Sd.rearrange("(c p) d -> p c d", p=P)).then_inc(s_weights, 16)

            def load_gate_up(c, done):
                for w, src in enumerate((Wg, Wu)):
                    for e in range(0, E, E // 2):
                        sp.dma_start(Wgu_sb[c][:, e:e + E // 2, w * F:(w + 1) * F],
                                     src[e:e + E // 2, c * P:(c + 1) * P, :].rearrange("e p f -> p e f")).then_inc(done, 16)
            with sp.Fori(1, NP) as p:
                for par in range(2):
                    b = p * 2 + par
                    sp.wait_ge(s_x, b * 16)
                    load_x(b)
                    sp.wait_ge(s_pv, b * TPB - TPB)
                    load_mem(b, par)

            sp.wait_ge(s_scored, NT)
            sp.wait_ge(s_pv, NT)
            load_gate_up(1, s_late)
            load_gate_up(0, s_late)
            sp.dma_start(Wd_sb[:], Wd.rearrange("e p d -> p e d")).then_inc(s_late, 16)

            sp.wait_ge(s_zero, 1)
            sp.wait_ge(s_plan, PADS_PLANNED)
            for e in range(E):
                row = sp.value_load(pad_row[0:1, e:e + 1], min_val=0, max_val=(E - 1) * EROWS + B * T)
                sp.dma_start(expert_in[bass.ds(row, P), :], zero_rows).then_inc(s_pad, 16)
            for q in range(2):
                sp.wait_ge(s_scat[q], NP * TPB * 2 * 16)
            sp.wait_ge(s_pad, E * 16)
            sp.wait_ge(s_plan, TILES_PLANNED)

            def load_rows(i, r):
                row = sp.value_load(tile_row[0:1, bass.ds(i, 1)], min_val=0, max_val=(E - 1) * EROWS + B * T)
                sp.dma_start(xin[:, r, :], expert_in[bass.ds(row, P), :]).then_inc(s_ein[r], 16)

            for i in range(RING):
                load_rows(i, i)
            with sp.Fori(1, MT // RING) as p:
                for r in range(RING):
                    sp.wait_ge(s_eturn, p * RING + (r + 1 - RING))
                    load_rows(p * RING + r, r)
            with sp.Fori(0, NT // TPB) as p:
                sp.wait_ge(s_final, p * (2 * TPB) + 2 * TPB)
                sp.dma_start(out_t[:, bass.ds(p * TPB, TPB), :], res[:, bass.ds(p * TPB, TPB), :]).then_inc(s_out, 16)
            sp.wait_ge(s_out, NT // TPB * 16)

        @block.gpsimd
        def _(pool):
            nc.gpsimd.memset(ident[:], 0.0).then_inc(s_const, 1)
            nc.gpsimd.memset(ones[:], 1.0).then_inc(s_const, 1)
            nc.gpsimd.memset(eps[:], LN_EPS).then_inc(s_const, 1)
            nc.gpsimd.memset(minus_half[:], -0.5).then_inc(s_const, 1)
            nc.gpsimd.memset(cum[:], 0.0).then_inc(s_const, 1)
            nc.gpsimd.memset(mem[:, :, :, D:D + 1], 1.0).then_inc(s_const, 1)
            nc.gpsimd.iota(iotaE[:], pattern=[[1, E]], base=0, channel_multiplier=0,
                           allow_small_or_imprecise_dtypes=True).then_inc(s_const, 1)
            nc.gpsimd.iota(ebase[:], pattern=[[EROWS, E]], base=0, channel_multiplier=0,
                           allow_small_or_imprecise_dtypes=True).then_inc(s_const, 1)
            pool.wait_ge(s_const, 8)
            nc.gpsimd.affine_select(out=ident[:], in_=ident[:], compare_op=ALU.not_equal, fill=1.0, base=0,
                                    pattern=[[-1, P]], channel_multiplier=1).then_inc(s_const, 1)
            nc.gpsimd.affine_select(out=before[:], in_=ones[:], compare_op=ALU.is_ge, fill=0.0, base=-1,
                                    pattern=[[1, P]], channel_multiplier=-1).then_inc(s_const, 1)

            def rstd_of(mv, to, stats_sem, n, done, k):
                pool.wait_ge(stats_sem, n)
                nc.gpsimd.tensor_tensor(to[:], mv[:, :, 1], eps[:], ALU.add).then_inc(done, 1)
                pool.wait_ge(done, k)
                nc.gpsimd.tensor_tensor(to[:], to[:], minus_half[:], ALU.pow).then_inc(done, 1)

            def add_bias(b):
                pool.wait_ge(s_xn, b * TPB + TPB)
                rb = res[:, bass.ds(b * TPB, TPB), :]
                nc.gpsimd.tensor_tensor(rb, rb, out_bias[:, None, :].to_broadcast([P, TPB, D]), ALU.add).then_inc(s_bias, 1)

            rstd_of(meanvar, rstd, s_ln, 2 * TPB, s_lnp, 1)
            pool.wait_ge(s_setup_c, SETUP_COPIES)
            add_bias(0)

            def step(t, b, j, par):
                if live(t, 2, NT):
                    pool.wait_ge(s_exp, t * 2 - 2)
                    nc.gpsimd.tensor_tensor(prob, prob, rest[:, j % 2, :], ALU.subtract).then_inc(s_masked, 1)
                if isinstance(b, int) and b == B + 1 and j == 0:
                    pool.wait_ge(s_pv, NT)
                    nc.gpsimd.iota(iota_t, pattern=[[1, MT]], base=0, channel_multiplier=0,
                                   allow_small_or_imprecise_dtypes=True).then_inc(s_iota, 1)
                if j == 1 and live(b, -1, B):
                    rstd_of(meanvar, rstd, s_ln, b * 8 + 16, s_lnp, b * 2 + 3)
                if j == 2 and live(b, 2, B):
                    pool.wait_ge(s_route, b * RK - 2 * RK + 15)
                    for n in range(TPB):
                        if n or since(b, 3):
                            pool.wait_ge(s_cum, b * 5 - 10 + n)
                        nc.gpsimd.tensor_tensor(cum[:, n + 1, :], cum[:, n, :], chosen[:, n, :], ALU.add).then_inc(s_cum, 1)
                if j in (1, 2) and live(b, 2, B):
                    h = j - 1
                    n0 = b * 6 - 12 + 3 * h
                    pool.wait_ge(s_sact, b * 2 - 4 + h + 1)
                    nc.gpsimd.tensor_tensor(gateact[:, 0, :], gateact[:, 0, :], gateact[:, 1, :], ALU.mult).then_inc(s_hid, 1)
                    pool.wait_ge(s_hid, n0 + 1)
                    nc.gpsimd.tensor_tensor(gateact[:, 0, :], gateact[:, 0, :], gateact[:, 1, :], ALU.add).then_inc(s_hid, 1)
                    pool.wait_ge(s_hid, n0 + 2)
                    if since(b, 3):
                        pool.wait_ge(s_down, b - 2)
                    nc.gpsimd.tensor_tensor(hid[:, h, :], gateact[:, 0, :], gateact[:, 2, :], ALU.mult).then_inc(s_hid, 1)
                if j == 2 and live(b, -1, B):
                    add_bias(b + 1)
                if j == 3 and live(b, 1, B):
                    rstd_of(meanvar2, rstd2, s_ln2, b * 8, s_ln2p, b * 2 - 1)
                if j == 3 and live(b, 2, B):
                    pool.wait_ge(s_cum, b * 5 - 10 + TPB)
                    pool.wait_ge(s_rankc, b - 1)
                    pool.sem_inc(s_held["pool"], 1)
                    nc.gpsimd.tensor_copy(cum[:, 0, :], cum[:, TPB, :]).then_inc(s_cum, 1)
                    pool.wait_ge(s_route, b * RK - RK)
                    pool.sem_inc(s_held["pool"], 1)
                    for n in range(TPB):
                        for k in range(2):
                            nc.gpsimd.indirect_dma_start(
                                out=expert_in[:, :], out_offset=bass.IndirectOffsetOnAxis(ap=slot_i[:, par, n, k:k + 1], axis=0),
                                in_=xn2[:, par, n, :], in_offset=None).then_inc(s_scat[par], 16)
                    pool.wait_ge(s_down, b - 1)
                    rb = res[:, bass.ds(b * TPB - 2 * TPB, TPB), :]
                    nc.gpsimd.tensor_tensor(rb, rb, down[:], ALU.add).then_inc(s_shared, 1)

            walk(pool, step)

            for r in range(RING):
                pool.wait_ge(s_ystore[r], MT // RING * 16)
            with pool.Fori(0, NT // (2 * TPB)) as p:
                for h in range(2):
                    pool.wait_ge(s_gidx, p * 2 + h + 1)
                    pool.sem_inc(s_held["pool"], 1)
                    for r in range(TPB):
                        for k in range(2):
                            nc.gpsimd.indirect_dma_start(
                                out=gath[:, h * TPB + r, k, :], out_offset=None, in_=expert_out[:, :],
                                in_offset=bass.IndirectOffsetOnAxis(ap=gidx[:, h, r, k:k + 1], axis=0)).then_inc(s_gath[h * TPB + r], 16)

        @block.scalar
        def _(act):
            turn = Count()

            def take():
                act.wait_ge(s_turn, turn.next())
                return turnP[(turn.n - 1) % 2]

            def signal(to):
                act.wait_ge(s_turnread, turn.now())
                act.sem_inc(to, 1)

            act.wait_ge(s_bcol, 1)
            nc.scalar.activation(bcols[:].rearrange("p n c -> p (n c)"), outP[:, 0:3 * DC], ACT.Copy).then_inc(s_bcol, 1)
            act.wait_ge(s_setup_p, 1)
            nc.scalar.activation(WoT_sb, turnP[0][:].rearrange("p (c n) -> p c n", c=DC), ACT.Copy).then_inc(s_setup_c, 1)
            act.wait_ge(s_setup_p, 2)
            nc.scalar.activation(Aqk[:], turnP[1][:].rearrange("p (c n) -> p c n", c=DC), ACT.Copy).then_inc(s_setup_c, 1)
            act.wait_ge(s_setup_p, 3)
            nc.scalar.activation(a_bias[:], pvP[:, 0:DC], ACT.Copy, scale=SCALE).then_inc(s_setup_c, 1)
            nc.scalar.activation(w_rowc[:], pvP[:, 8:8 + DC], ACT.Copy).then_inc(s_setup_c, 1)
            nc.scalar.activation(rowc0[:], pvP[:, 16:17], ACT.Copy, scale=SCALE).then_inc(s_setup_c, 1)
            act.wait_ge(s_setup_p, 4)
            nc.scalar.activation(Cvo[:], turnP[0][:].rearrange("p (c n) -> p c n", c=DC), ACT.Copy).then_inc(s_setup_c, 1)
            act.wait_ge(s_setup_p, 5)
            nc.scalar.activation(out_bias[:], outP[:, 0:D], ACT.Copy).then_inc(s_setup_c, 1)

            def copy_memT(h, q):
                for g in GROUPS:
                    w = sum(rows(c) for c in g)
                    src = take()
                    nc.scalar.activation(memT[:, q, h, g[0] * P:g[0] * P + w], src[:, 0:w], ACT.Copy).then_inc(s_turnread, 1)

            def copy_xnT():
                for c in range(DC):
                    src = take()
                    nc.scalar.activation(xnT[:, c, :], src[:], ACT.Copy).then_inc(s_turnread, 1)

            def copy_qT(b, q):
                for c in range(DC):
                    src = take()
                    nc.scalar.activation(qT[:, c, :], src[:], ACT.Identity, scale=SCALE,
                                         bias=a_bias[:, c:c + 1]).then_inc(s_turnread, 1)
                src = take()
                nc.scalar.activation(rowc[:], src[:, 0:TPB], ACT.Identity, scale=SCALE, bias=rowc0[:, 0:1]).then_inc(s_turnread, 1)

            act.wait_ge(s_setup_c, SETUP_COPIES)
            for h in range(DC):
                copy_memT(h, 0)
            copy_xnT()
            copy_qT(0, 0)

            def step(t, b, j, par):
                if live(t, 2, NT):
                    act.wait_ge(s_topk, t * TK - TK)
                    nc.scalar.activation(rest[:, j % 2, :], rest[:, j % 2, :], ACT.Exp, bias=negmax[:, j % 2:j % 2 + 1]).then_inc(s_exp, 1)
                if live(t, 0, NT):
                    if j == 0:
                        act.wait_ge(s_turnread, turn.now())
                    act.wait_ge(s_scored, t + 1)
                    if since(t, 2):
                        act.wait_ge(s_topk, t * TK - 2 * TK + 2)
                        act.wait_ge(s_exp, t * 2 - 3)
                    nc.scalar.activation(score[:, j % 2, :], scoreP[:, 0:S], ACT.Identity,
                                         bias=rowc[:, j:j + 1]).then_inc(s_score, 1)
                if live(t, 3, NT):
                    src = take()
                    if since(t, 4):
                        act.wait_ge(s_proj, t - 3)
                    nc.scalar.activation(attT[:], src[:, 0:D].rearrange("p (c n) -> p c n", c=DC), ACT.Copy).then_inc(s_turnread, 1)
                if j == 0 and live(b, 2, B):
                    for c in range(DC):
                        src = take()
                        nc.scalar.activation(xn2T[:, c, :], src[:], ACT.Copy).then_inc(s_turnread, 1)
                    src = take()
                    nc.scalar.activation(logit[:], src[:, 0:TPB * E].rearrange("p (j e) -> p j e", e=E),
                                         ACT.Copy).then_inc(s_turnread, 1)
                    signal(s_logit)
                if live(t, 2, NT):
                    for g in GROUPS:
                        src = take()
                        if g[0] == 0 and since(t, 3):
                            act.wait_ge(s_pv, t - 2)
                        r = rows(g[-1])
                        nc.scalar.activation(probT[0:r, g[0]:g[-1] + 1, :],
                                             src[0:r, 0:len(g) * P].rearrange("p (c n) -> p c n", n=P),
                                             ACT.Copy).then_inc(s_turnread, 1)
                if j == 2 and live(b, 2, B):
                    src = take()
                    nc.scalar.activation(rank[:], src[:, 0:TPB * E].rearrange("p (j e) -> p j e", e=E),
                                         ACT.Copy).then_inc(s_turnread, 1)
                    signal(s_rankc)
                if live(t, 1, NT):
                    act.wait_ge(s_neg, t)
                    q = (j - 1) % 2
                    nc.scalar.activation(prob, score[:, q, :], ACT.Exp, bias=negmax[:, q:q + 1]).then_inc(s_exp, 1)
                if j == 1 and live(b, 2, B):
                    act.wait_ge(s_route, b * RK - 2 * RK + 2)
                    for n in range(TPB):
                        nc.scalar.activation(rexp[:, n, :], logit[:, n, :], ACT.Exp, bias=lneg[:, n:n + 1],
                                             accum_out=rexps[:, n:n + 1]).then_inc(s_rexp, 1)
                if live(t, 2, NT):
                    act.wait_ge(s_pv, t - 1)
                    if since(t, 4):
                        act.wait_ge(s_proj, t - 3)
                        act.wait_ge(s_rsum, t - 3)
                    nc.scalar.activation(att[:, j % 2, :], pvP[:, 0:D + 1], ACT.Copy).then_inc(s_att, 1)
                if j in (0, 1) and live(b, 2, B):
                    h = j
                    src = take()
                    if h:
                        act.wait_ge(s_hid, b * 6 - 12 + 3)
                    elif since(b, 3):
                        act.wait_ge(s_shared, b - 2)
                    nc.scalar.activation(gateact[:, 0, :], src[:], ACT.Tanh, scale=0.5)
                    nc.scalar.activation(gateact[:, 1, :], src[:], ACT.Copy).then_inc(s_turnread, 1)
                    src = take()
                    nc.scalar.activation(gateact[:, 2, :], src[:], ACT.Copy, scale=0.5).then_inc(s_turnread, 1)
                    signal(s_sact)
                if j in (2, 3) and live(b, -1, B):
                    copy_memT(j - 2, (par + 1) % 2)
                if j == 2 and live(b, -1, B):
                    copy_xnT()
                if j == 3 and live(b, -1, B):
                    copy_qT(b + 1, (par + 1) % 2)
                if j == 2 and live(b, 2, B):
                    for n in range(0, TPB, 2):
                        src = take()
                        if n == 0:
                            act.wait_ge(s_hid, b * 6 - 6)
                        nc.scalar.activation(down[:, n:n + 2, :], src[:].rearrange("p (c n) -> p c n", c=2),
                                             ACT.Copy).then_inc(s_turnread, 1)
                    signal(s_down)

            walk(act, step, turn)

            def estep(i, r):
                if live(i, 2, MT):
                    q = r % 2
                    act.wait_ge(s_gu, i - 1)
                    if since(i, 4):
                        act.wait_ge(s_eh, i * 2 - 6)
                    nc.scalar.activation(etanh[:, q, :], guP[q][:, 0:F], ACT.Tanh, scale=0.5).then_inc(s_eact, 1)
                if live(i, 0, MT):
                    act.wait_ge(s_eturn, i + 1)
                    nc.scalar.activation(xinT[:, r % 2], turnP[r % 2][:, 0:D].rearrange("p (c n) -> p c n", c=DC),
                                         ACT.Copy).then_inc(s_eturnc, 1)
                if live(i, 5, MT):
                    q = (r - 5) % RING
                    act.wait_ge(s_y, i - 4)
                    act.dma_start(expert_out[bass.ds(i * P - 5 * P, P), :], yout[:, q % (RING // 2), :]).then_inc(s_ystore[q], 16)
                if live(i, 4, MT):
                    q = (r - 4) % RING
                    act.wait_ge(s_ydone, i - 3)
                    if since(i, RING // 2 + 4):
                        h = (q + RING // 2) % RING
                        act.wait_ge(s_ystore[h], (i - 4 - RING // 2 - h) * 2 + 16)
                    nc.scalar.activation(yout[:, q % (RING // 2), :], yP[q % 2][:, 0:D], ACT.Copy).then_inc(s_y, 1)

            ewalk(act, estep)

        @block.vector
        def _(dve):
            def stats1(b):
                dve.wait_ge(s_x, b * 16 + 16)
                if since(b, 1):
                    dve.wait_ge(s_xn, b * TPB)
                dve.sem_inc(s_held["dve"], 1)
                for n in range(TPB):
                    nc.vector.bn_stats(stats[:, n, :], res[:, b * TPB + n, :]).then_inc(s_ln, 1)
                dve.wait_ge(s_ln, b * 8 + TPB)
                dve.sem_inc(s_held["dve"], 1)
                for n in range(TPB):
                    nc.vector.bn_aggr(meanvar[:, n, :], stats[:, n, :]).then_inc(s_ln, 1)

            def normed1(b):
                dve.wait_ge(s_lnp, b * 2 + 2)
                if since(b, 1):
                    dve.wait_ge(s_scored, b * TPB - TPB + 1)
                for n in range(TPB):
                    nc.vector.tensor_scalar(xn[:, n, :], res[:, b * TPB + n, :], meanvar[:, n, 0:1], rstd[:, n:n + 1],
                                            ALU.subtract, ALU.mult).then_inc(s_xn, 1)

            dve.wait_ge(s_const, 10)
            dve.wait_ge(s_bcol, 2)
            for c in range(DC):
                nc.vector.tensor_scalar(bq_wide[:, c, :], ones[:], bcols[:, 0, c:c + 1], None, ALU.mult).then_inc(s_wide, 1)
                nc.vector.tensor_scalar(bv_wide[:, c, :], ones[:], bcols[:, 2, c:c + 1], None, ALU.mult).then_inc(s_wide, 1)
            stats1(0)
            normed1(0)

            def step(t, b, j, par):
                if live(b, 1, B) and j == 3:
                    pp = (par + 1) % 2
                    dve.wait_ge(s_ln2p, b * 2)
                    if since(b, 3):
                        dve.wait_ge(s_scat[pp], (b - 1 - pp) * (TPB * 16))
                    for n in range(TPB):
                        nc.vector.tensor_scalar(xn2[:, pp, n, :], res[:, b * TPB - TPB + n, :],
                                                meanvar2[:, n, 0:1], rstd2[:, n:n + 1],
                                                ALU.subtract, ALU.mult).then_inc(s_xn2, 1)
                r0 = b * RK - 2 * RK
                mt = bass.ds(b * TPB - 2 * TPB, TPB)
                def between():
                    if live(t, 3, NT):
                        q, n2 = (j + 1) % 2, (j + 1) % TPB
                        dve.wait_ge(s_att, t - 2)
                        if since(t, 5):
                            dve.wait_ge(s_res, t - 4)
                        nc.vector.reciprocal(rsum[:, q:q + 1], att[:, q, D:D + 1]).then_inc(s_rsum, 1)
                        dve.wait_ge(s_rsum, t - 2)
                        dve.wait_ge(s_proj, t - 2)
                        if j == 3:
                            dve.wait_ge(s_bias, b + 1)
                        r = res[:, t - 3, :]
                        nc.vector.scalar_tensor_tensor(out=r, in0=outP[:, 0:D], scalar=rsum[:, q:q + 1], in1=r,
                                                       op0=ALU.mult, op1=ALU.add).then_inc(s_res, 1)
                        dve.wait_ge(s_res, t - 2)
                        dve.sem_inc(s_held["dve"], 1)
                        nc.vector.bn_stats(stats2[:, n2, :], r).then_inc(s_ln2, 1)
                        dve.wait_ge(s_ln2, t * 2 - 5)
                        if j == 3 and live(b, 1, B):
                            dve.wait_ge(s_xn2, b * TPB)
                        dve.sem_inc(s_held["dve"], 1)
                        nc.vector.bn_aggr(meanvar2[:, n2, :], stats2[:, n2, :]).then_inc(s_ln2, 1)
                    if j == 0 and live(b, -1, B):
                        stats1(b + 1)
                    if j == 0 and live(b, 2, B):
                        dve.wait_ge(s_logit, b - 1)
                        nc.vector.tensor_reduce(lneg[:], logit[:], AX_X, ALU.max).then_inc(s_route, 1)
                        dve.wait_ge(s_route, r0 + 1)
                        nc.vector.tensor_scalar(lneg[:], lneg[:], -1.0, None, ALU.mult).then_inc(s_route, 1)
                    if j == 2 and live(b, 2, B):
                        dve.wait_ge(s_rankc, b - 1)
                        nc.vector.tensor_tensor(rank[:], rank[:], ebase[:, None, :].to_broadcast([P, TPB, E]), ALU.add).then_inc(s_route, 1)
                        dve.wait_ge(s_route, r0 + 16)
                        nc.vector.tensor_tensor(onehot[:], onehot[:], rank[:, :, None, :].to_broadcast([P, TPB, 2, E]),
                                                ALU.mult).then_inc(s_route, 1)
                        dve.wait_ge(s_route, r0 + 17)
                        nc.vector.tensor_reduce(slot[:, mt, :], onehot[:], AX_X, ALU.add).then_inc(s_route, 1)
                        dve.wait_ge(s_route, r0 + 18)
                        if since(b, 4):
                            dve.wait_ge(s_scat[par], (b - 2 - par) * (TPB * 16))
                        dve.sem_inc(s_held["dve"], 1)
                        nc.vector.tensor_copy(slot_i[:, par, :, :], slot[:, mt, :]).then_inc(s_route, 1)


                if j == 1 and live(b, -1, B):
                    normed1(b + 1)
                if j == 1 and live(b, 2, B):
                    dve.wait_ge(s_rexp, b * TPB - TPB)
                    nc.vector.reciprocal(rinv[:], rexps[:]).then_inc(s_route, 1)
                    dve.sem_inc(s_held["dve"], 1)
                    for n in range(TPB):
                        nc.vector.max(rtop[:, n, :], rexp[:, n, :]).then_inc(s_route, 1)
                    dve.wait_ge(s_route, r0 + 7)
                    dve.sem_inc(s_held["dve"], 1)
                    for n in range(TPB):
                        nc.vector.max_index(ridx[:, n, :], rtop[:, n, :], rexp[:, n, :]).then_inc(s_route, 1)
                    nc.vector.tensor_tensor(gates[:, mt, :], rtop[:, :, 0:2], rinv[:, :, None].to_broadcast([P, TPB, 2]),
                                            ALU.mult).then_inc(s_route, 1)
                    dve.wait_ge(s_route, r0 + 12)
                    nc.vector.tensor_copy(choice[:, mt, :], ridx[:, :, 0:2]).then_inc(s_route, 1)
                    dve.wait_ge(s_route, r0 + 13)
                    nc.vector.tensor_tensor(onehot[:], iotaE[:, None, None, :].to_broadcast([P, TPB, 2, E]),
                                            choice[:, mt, :, None].to_broadcast([P, TPB, 2, E]), ALU.is_equal).then_inc(s_route, 1)
                    dve.wait_ge(s_route, r0 + 14)
                    if since(b, 3):
                        dve.wait_ge(s_rankc, b - 2)
                    nc.vector.tensor_tensor(chosen[:], onehot[:, :, 0, :], onehot[:, :, 1, :], ALU.add).then_inc(s_route, 1)

                if live(t, 0, NT):
                    q, k0 = j % 2, t * TK
                    dve.wait_ge(s_score, t + 1)
                    if since(t, 2):
                        dve.wait_ge(s_exp, t * 2 - 2)
                        dve.wait_ge(s_masked, t - 1)
                    dve.sem_inc(s_held["dve"], 1)
                    nc.vector.max(best[:, q, 0:8], score[:, q, :]).then_inc(s_topk, 1)
                    dve.wait_ge(s_topk, k0 + 1)
                    nc.vector.tensor_scalar(negmax[:, q:q + 1], best[:, q, 0:1], -1.0, None, ALU.mult).then_inc(s_neg, 1)
                    nc.vector.match_replace(rest[:, q, :], best[:, q, 0:8], score[:, q, :], GONE).then_inc(s_topk, 1)
                    between()
                    for n in range(1, ROUNDS):
                        b8 = best[:, q, 8 * n:8 * n + 8]
                        dve.wait_ge(s_topk, k0 + 2 * n)
                        dve.sem_inc(s_held["dve"], 1)
                        nc.vector.max(b8, rest[:, q, :]).then_inc(s_topk, 1)
                        dve.wait_ge(s_topk, k0 + 2 * n + 1)
                        dve.sem_inc(s_held["dve"], 1)
                        nc.vector.match_replace(rest[:, q, :], b8, rest[:, q, :], GONE).then_inc(s_topk, 1)
                else:
                    between()

            walk(dve, step)

            done = Count()

            def then(ins):
                ins.then_inc(s_plan, 1)
                dve.wait_ge(s_plan, done.next())

            dve.wait_ge(s_count, 1)
            dve.wait_ge(s_pv, NT)
            nc.vector.memset(zero_rows, 0.0).then_inc(s_zero, 1)
            then(nc.vector.tensor_copy(count, scoreP[:, 0:E]))
            then(nc.vector.tensor_tensor(padf, count, ebase[:], ALU.add))
            then(nc.vector.tensor_copy(pad_row[:], padf))
            assert done.n == PADS_PLANNED
            then(nc.vector.tensor_scalar(tiles_i[:], count, 1.0 / P, (P - 1.0) / P - 0.5 + 0.5 / P, ALU.mult, ALU.add))
            then(nc.vector.tensor_copy(tiles, tiles_i[:]))
            then(nc.vector.tensor_copy(incl[0], tiles))
            n, a = 1, 0
            while n < E:
                then(nc.vector.tensor_copy(incl[1 - a][:, 0:n], incl[a][:, 0:n]))
                then(nc.vector.tensor_tensor(incl[1 - a][:, n:E], incl[a][:, n:E], incl[a][:, 0:E - n], ALU.add))
                n, a = 2 * n, 1 - a
            upto = incl[a]
            then(nc.vector.tensor_scalar(lastt, upto[:, E - 1:E], -1.0, None, ALU.add))
            dve.wait_ge(s_iota, 1)
            then(nc.vector.tensor_scalar(tidx, iota_t, lastt, None, ALU.min))
            then(nc.vector.tensor_tensor(passed, tidx[:, :, None].to_broadcast([P, MT, E]),
                                         upto[:, None, :].to_broadcast([P, MT, E]), ALU.is_ge))
            then(nc.vector.tensor_reduce(trow, passed, AX_X, ALU.add))
            then(nc.vector.tensor_copy(tile_expert, trow))
            then(nc.vector.tensor_scalar(gap, tiles, -float(P), float(EROWS), ALU.mult, ALU.add))
            then(nc.vector.tensor_tensor(passed, passed, gap[:, None, :].to_broadcast([P, MT, E]), ALU.mult))
            then(nc.vector.tensor_reduce(trow, passed, AX_X, ALU.add))
            then(nc.vector.scalar_tensor_tensor(out=tile_row, in0=tidx, scalar=float(P), in1=trow, op0=ALU.mult, op1=ALU.add))
            assert done.n == TILES_PLANNED
            then(nc.vector.tensor_tensor(excl, upto, tiles, ALU.subtract))
            then(nc.vector.scalar_tensor_tensor(out=shift, in0=excl, scalar=float(P), in1=ebase[:], op0=ALU.mult, op1=ALU.subtract))
            then(nc.vector.tensor_tensor(shifted, iotaE[:, None, :].to_broadcast([P, 2 * NT, E]),
                                         choice[:].rearrange("p t k -> p (t k)")[:, :, None].to_broadcast([P, 2 * NT, E]),
                                         ALU.is_equal))
            then(nc.vector.tensor_tensor(shifted, shifted, shift[:, None, :].to_broadcast([P, 2 * NT, E]), ALU.mult))
            then(nc.vector.tensor_reduce(yrow, shifted, AX_X, ALU.add))
            then(nc.vector.tensor_tensor(yrow_i.rearrange("p t k -> p (t k)"), yrow,
                                         slot[:].rearrange("p t k -> p (t k)"), ALU.add))
            assert done.n == PLAN

            def estep(i, r):
                if live(i, 2, MT):
                    q = r % 2
                    g, u = guP[q][:, 0:F], guP[q][:, F:2 * F]
                    dve.wait_ge(s_eact, i - 1)
                    if since(i, 4):
                        dve.wait_ge(s_ehT, i - 3)
                    nc.vector.scalar_tensor_tensor(out=ehid[:, q, :], in0=etanh[:, q, :], scalar=1.0, in1=g,
                                                   op0=ALU.add, op1=ALU.mult).then_inc(s_eh, 1)
                    dve.wait_ge(s_eh, i * 2 - 3)
                    nc.vector.scalar_tensor_tensor(out=ehid[:, q, :], in0=ehid[:, q, :], scalar=0.5, in1=u,
                                                   op0=ALU.mult, op1=ALU.mult).then_inc(s_eh, 1)
                if live(i, 3, MT):
                    q = (r - 3) % 2
                    dve.wait_ge(s_ehT, i - 2)
                    if since(i, 5):
                        dve.wait_ge(s_ydone, i - 4)
                    nc.vector.tensor_copy(ehidT[:, q, :], ehTP[q][:, 0:P]).then_inc(s_ehTc, 1)

            ewalk(dve, estep)

            dve.wait_ge(s_shared, B)
            def indices(p, h):
                nc.vector.tensor_copy(gidx[:, h, :, :], yrow_i[:, bass.ds(p * 2 * TPB + h * TPB, TPB), :]).then_inc(s_gidx, 1)

            def add_up(p, h):
                for r in range(TPB):
                    tile = p * 2 * TPB + h * TPB + r
                    rr = res[:, tile, :]
                    dve.wait_ge(s_gath[h * TPB + r], p * 32 + 32)
                    for k in range(2):
                        if k:
                            dve.wait_ge(s_final, tile * 2 + 1)
                        nc.vector.scalar_tensor_tensor(out=rr, in0=gath[:, h * TPB + r, k, :], scalar=gates[:, tile, k:k + 1], in1=rr,
                                                       op0=ALU.mult, op1=ALU.add).then_inc(s_final, 1)
                dve.wait_ge(s_final, p * (4 * TPB) + (h + 1) * 2 * TPB)

            for h in range(2):
                indices(0, h)
            with dve.Fori(0, NT // (2 * TPB) - 1) as p:
                for h in range(2):
                    add_up(p, h)
                    dve.sem_inc(s_held["dve"], 1)
                    indices(p + 1, h)
            for h in range(2):
                add_up(NT // (2 * TPB) - 1, h)

        @block.tensor
        def _(pe):
            pe.wait_ge(s_const, 10)
            pe.wait_ge(s_small, 16 * 8)
            pe.transpose(outP[:, 0:3 * DC], brows, ident[0:3 * DC, 0:3 * DC]).then_inc(s_bcol, 1)
            for oc in range(DC):
                for c in range(DC):
                    mm = pe.transpose(turnP[0][:, oc * D + c * P:oc * D + (c + 1) * P], Wo_sb[:, c, oc * P:(oc + 1) * P], ident[:])
            mm.then_inc(s_setup_p, 1)

            def product(to, terms):
                for n, (lhsT, rhs) in enumerate(terms):
                    mm = pe.matmul(to, lhsT, rhs, start=(n == 0), stop=(n == len(terms) - 1))
                return mm

            for c in range(DC):
                mm = product(turnP[1][:, c * D:(c + 1) * D], [(Wq_sb[:, o, c * P:(c + 1) * P], Wk_sb[:, o, :]) for o in range(DC)])
            mm.then_inc(s_setup_p, 1)
            pe.wait_ge(s_bcol, 2)
            pe.wait_ge(s_wide, 2 * DC)
            for c in range(DC):
                product(pvP[:, c:c + 1], [(Wk_sb[:, o, c * P:(c + 1) * P], bcols[:, 0, o:o + 1]) for o in range(DC)])
                product(pvP[:, 8 + c:9 + c], [(Wq_sb[:, o, c * P:(c + 1) * P], bcols[:, 1, o:o + 1]) for o in range(DC)])
            product(pvP[:, 16:17], [(bq_wide[:, o, :], bcols[:, 1, o:o + 1]) for o in range(DC)]).then_inc(s_setup_p, 1)
            pe.wait_ge(s_setup_c, 1)
            for c in range(DC):
                mm = product(turnP[0][:, c * D:(c + 1) * D], [(Wv_sb[:, o, c * P:(c + 1) * P], WoT_sb[:, o, :]) for o in range(DC)])
            mm.then_inc(s_setup_p, 1)
            product(outP[:, 0:D], [(bv_wide[:, o, :], WoT_sb[:, o, :]) for o in range(DC)]
                    + [(ones[0:1, :], bo_row[0:1, :])]).then_inc(s_setup_p, 1)
            pe.wait_ge(s_setup_c, SETUP_COPIES)

            turn = Count()

            def give():
                n = turn.next()
                if not isinstance(n, int) or n > 2:
                    pe.wait_ge(s_turnread, turn.now(2))
                return turnP[(turn.n - 1) % 2]

            def turn_mem(b, h, q):
                if h == 0:
                    pe.wait_ge(s_mem[q], (b - q) * 16 + 32)
                for g in GROUPS:
                    to = give()
                    for n, c in enumerate(g):
                        mm = pe.transpose(to[:, n * P:n * P + rows(c)], mem[0:rows(c), q, c, h * P:(h + 1) * P],
                                          ident[0:rows(c), 0:rows(c)])
                    mm.then_inc(s_turn, 1)

            def turn_xn(src, ready, n0):
                pe.wait_ge(ready, n0)
                for c in range(DC):
                    to = give()
                    for n in range(TPB):
                        mm = pe.transpose(to[:, n * P:(n + 1) * P], src(n, c), ident[:])
                    mm.then_inc(s_turn, 1)

            def query(b):
                pe.wait_ge(s_turnread, turn.now())
                for c in range(DC):
                    product(give()[:], [(Aqk[:, k, c * P:(c + 1) * P], xnT[:, k, :]) for k in range(DC)]).then_inc(s_turn, 1)
                to = give()
                for n in range(TPB):
                    mm = product(to[:, n:n + 1], [(xnT[:, k, n * P:(n + 1) * P], w_rowc[:, k:k + 1]) for k in range(DC)])
                mm.then_inc(s_turn, 1)

            def xn_part(n, c):
                return xn[:, n, c * P:(c + 1) * P]

            for h in range(DC):
                turn_mem(0, h, 0)
            turn_xn(xn_part, s_xn, TPB)
            query(0)

            def step(t, b, j, par):
                if live(t, 0, NT):
                    if j == 0:
                        pe.wait_ge(s_turnread, turn.now())
                    if since(t, 1):
                        pe.wait_ge(s_score, t)
                    for a, z in CHUNKS:
                        mm = product(scoreP[:, a:z], [(qT[:, k, j * P:(j + 1) * P], memT[:, par, k, a:z]) for k in range(DC)])
                    mm.then_inc(s_scored, 1)
                if live(t, 3, NT):
                    pe.wait_ge(s_att, t - 2)
                    to = give()
                    attT_copied = turn.now()
                    for c in range(DC):
                        mm = pe.transpose(to[:, c * P:(c + 1) * P], att[:, (j - 3) % 2, c * P:(c + 1) * P], ident[:])
                    mm.then_inc(s_turn, 1)
                if j == 0 and live(b, 2, B):
                    turn_xn(lambda n, c: xn2[:, par, n, c * P:(c + 1) * P], s_xn2, b * TPB - TPB)
                    pe.wait_ge(s_turnread, turn.now())
                    if isinstance(b, int) and b == 2 or not isinstance(b, int):
                        pe.wait_ge(s_weights, NWEIGHTS)
                    to = give()
                    for n in range(TPB):
                        mm = product(to[:, n * E:(n + 1) * E], [(xn2T[:, k, n * P:(n + 1) * P], Wr_sb[:, k, :]) for k in range(DC)])
                    mm.then_inc(s_turn, 1)
                def turn_prob(g):
                    to = give()
                    for n, c in enumerate(g):
                        mm = pe.transpose(to[0:rows(c), n * P:(n + 1) * P], prob[:, c * P:c * P + rows(c)], ident[:])
                    mm.then_inc(s_turn, 1)
                    return turn.now()

                copied = []
                if live(t, 2, NT):
                    pe.wait_ge(s_masked, t - 1)
                    copied = [turn_prob(g) for g in GROUPS[:2]]
                if live(t, 3, NT):
                    pe.wait_ge(s_turnread, attT_copied)
                    if since(t, 4):
                        pe.wait_ge(s_res, t - 3)
                    product(outP[:, 0:D], [(attT[:, k, :], Cvo[:, k, :]) for k in range(DC)]).then_inc(s_proj, 1)
                if isinstance(b, int) and b == B + 1 and j == 2:
                    pe.wait_ge(s_score, NT)
                    pe.wait_ge(s_cum, 5 * B - 5 + TPB)
                    product(scoreP[:, 0:E], [(ones[:], cum[:, TPB, :])]).then_inc(s_count, 1)
                if live(t, 2, NT):
                    mq = par if j >= 2 else (par + 1) % 2
                    if since(t, 3):
                        pe.wait_ge(s_att, t - 2)
                    for i, g in enumerate(GROUPS):
                        pe.wait_ge(s_turnread, copied[i])
                        for c in g:
                            mm = pe.matmul(pvP[:, 0:D + 1], probT[0:rows(c), c, :], mem[0:rows(c), mq, c, :],
                                           start=(c == 0), stop=(c == SC - 1))
                        if i + 2 < NG:
                            copied.append(turn_prob(GROUPS[i + 2]))
                    mm.then_inc(s_pv, 1)
                if j == 2 and live(b, 2, B):
                    pe.wait_ge(s_route, b * RK - 2 * RK + 15)
                    pe.wait_ge(s_cum, b * 5 - 10 + TPB)
                    product(give()[:, 0:TPB * E],
                            [(before[:], chosen[:].rearrange("p j e -> p (j e)")),
                             (ones[:], cum[:, 0:TPB, :].rearrange("p j e -> p (j e)"))]).then_inc(s_turn, 1)
                if j in (0, 1) and live(b, 2, B):
                    for w in range(2):
                        f = w * FS + j * P
                        product(give()[:], [(Sgu_sb[:, k, f:f + P], xn2T[:, k, :]) for k in range(DC)]).then_inc(s_turn, 1)
                if j in (2, 3) and live(b, -1, B):
                    turn_mem(b + 1, j - 2, (par + 1) % 2)
                if j == 2 and live(b, -1, B):
                    turn_xn(xn_part, s_xn, b * TPB + 2 * TPB)
                if j == 3 and live(b, -1, B):
                    query(b + 1)
                if j == 2 and live(b, 2, B):
                    pe.wait_ge(s_hid, b * 6 - 6)
                    for n in range(0, TPB, 2):
                        to = give()
                        for m in range(2):
                            mm = product(to[:, m * D:(m + 1) * D],
                                         [(hid[:, f, (n + m) * P:(n + m + 1) * P], Sd_sb[:, f, :]) for f in range(FC)])
                        mm.then_inc(s_turn, 1)

            walk(pe, step, turn)

            pe.wait_ge(s_turnread, turn.now())
            pe.wait_ge(s_plan, TILES_PLANNED)
            pe.wait_ge(s_res, NT)
            pe.wait_ge(s_late, 144)

            expert = {}

            def know(i, r, lag):
                if live(i, lag, MT) and r - lag not in expert:
                    expert[r - lag] = pe.value_load(tile_expert[0:1, bass.ds(i - lag, 1)], min_val=0, max_val=E - 1)

            def estep(i, r):
                if r == 0:
                    expert.clear()
                    know(i, r, 2)
                    know(i, r, 4)
                if live(i, 2, MT):
                    q = r % 2
                    e_gu = expert[r - 2]
                    pe.wait_ge(s_eturnc, i - 1)
                    if since(i, 4):
                        pe.wait_ge(s_eh, i * 2 - 6)
                    product(guP[q][:, 0:2 * F], [(xinT[:, q, k, :], Wgu_sb[k][:, bass.ds(e_gu, 1), :]) for k in range(DC)]).then_inc(s_gu, 1)
                if r < TURN - 1:
                    know(i + 1, r + 1, 2)
                    know(i + 1, r + 1, 4)
                if live(i, 0, MT):
                    pe.wait_ge(s_ein[r % RING], (i - r % RING) * 2 + 16)
                    if since(i, 2):
                        pe.wait_ge(s_eturnc, i - 1)
                    for c in range(DC):
                        mm = pe.transpose(turnP[r % 2][:, c * P:(c + 1) * P], xin[:, r % RING, c * P:(c + 1) * P], ident[:])
                    mm.then_inc(s_eturn, 1)
                if live(i, 4, MT):
                    q = r % 2
                    pe.wait_ge(s_ehTc, i - 3)
                    if since(i, 6):
                        pe.wait_ge(s_y, i - 5)
                    product(yP[q][:, 0:D], [(ehidT[:, q, :], Wd_sb[:, bass.ds(expert[r - 4], 1), :])]).then_inc(s_ydone, 1)
                if live(i, 3, MT):
                    q = (r - 3) % 2
                    pe.wait_ge(s_eh, i * 2 - 4)
                    if since(i, 5):
                        pe.wait_ge(s_ehTc, i - 4)
                    pe.transpose(ehTP[q][:, 0:P], ehid[:, q, :], ident[:]).then_inc(s_ehT, 1)

            ewalk(pe, estep)


_INS = ["x", "ctx_1024", "L0_xattn_Wq", "L0_xattn_bq", "L0_xattn_Wk", "L0_xattn_bk", "L0_xattn_Wv", "L0_xattn_bv",
        "L0_xattn_Wo", "L0_xattn_bo", "L0_ffn_Wr", "L0_ffn_Wg", "L0_ffn_Wu", "L0_ffn_Wd", "L0_ffn_Sg", "L0_ffn_Su", "L0_ffn_Sd"]


def kernel(**inputs):
    import numpy as _np
    import concourse.bacc as _bacc
    from concourse import mybir as _mybir
    from concourse.bass_utils import run_bass_kernel_spmd as _run

    nc = _bacc.Bacc("TRN2", target_bir_lowering=False, num_devices=1)
    arrays, args = {}, []
    for name in _INS:
        a = _np.ascontiguousarray(inputs[name])
        arrays[f"in_{name}_dram"] = a
        args.append(nc.dram_tensor(f"in_{name}_dram", a.shape, _mybir.dt.from_np(a.dtype), kind="ExternalInput").ap())
    shape = _np.shape(inputs["x"])
    args.append(nc.dram_tensor("out_0_dram", shape, _mybir.dt.float32, kind="ExternalOutput").ap())
    xattn_moe_kernel(nc, *args)
    r = _run(nc, [arrays], core_ids=[0])
    return r.results[0]["out_0_dram"]
```

```python
from contextlib import ExitStack

import concourse.bass as bass
from concourse import mybir

P = 128
F32 = mybir.dt.float32
BF16 = mybir.dt.bfloat16
I32 = mybir.dt.int32
U32 = mybir.dt.uint32
ALU = mybir.AluOpType
ACT = mybir.ActivationFunctionType
AX_X = mybir.AxisListType.X

TOP_K = 32
ROUNDS = TOP_K // 8
LN_EPS = 1e-5
GONE = -3.0e38
TPB = 4


class Count:

    def __init__(self):
        self.base, self.n = 0, 0

    def next(self):
        self.n += 1
        return self.now()

    def now(self, back=0):
        return self.base + (self.n - back)

    def at(self, base, n=0):
        self.base, self.n = base, n


def since(v, first):
    return not isinstance(v, int) or v >= first


def live(v, lag, n):
    return not isinstance(v, int) or 0 <= v - lag < n


def xattn_moe_kernel(nc, x, ctx_1024, Wq, bq, Wk, bk, Wv, bv, Wo, bo, Wr, Wg, Wu, Wd, Sg, Su, Sd, out):
    B, T, D = x.shape
    S = ctx_1024.shape[1]
    E, _, F = Wg.shape
    FS = Sg.shape[1]
    DC = D // P
    FC = FS // P
    NT = B * T // P
    SF = S // P
    SR = S - SF * P
    SC = SF + 1
    SCALE = float(D) ** -0.5
    assert T == TPB * P and D == 2 * P and F == P and FS == 2 * P and B % 4 == 0 and B >= 8 and 0 < SR < P
    EROWS = B * T + P
    MT = 2 * NT + E
    RING = 8
    BODY = 3 * RING
    assert MT % BODY == 0
    TC = -(-MT // P)
    assert TC * P <= 512
    GROUPS = [list(range(g, min(g + 4, SC))) for g in range(0, SC, 4)]
    NG = len(GROUPS)
    CHUNKS = [(c, min(c + 512, S)) for c in range(0, S, 512)]
    HALF = 2 * 512
    HALVINGS = D.bit_length() - 1
    TK = 2 * ROUNDS
    RK = 19
    PREP_TURNS = DC * NG + 2 * DC
    BATCH_TURNS = TPB * (NG + 1) + PREP_TURNS + DC + 2 + 1

    MEM_TURNS = DC * NG
    MEM_BESIDE, MEM_LATE = ((0,), (1,), (2, 3), (4, 5)), (6, 7)
    assert NG == 4 and DC == 2 and TPB == 2 * DC

    def rows(c):
        return P if c < SF else SR

    x_t = x.rearrange("b (j p) d -> p (b j) d", p=P)
    out_t = out.rearrange("b (j p) d -> p (b j) d", p=P)

    with ExitStack() as ctx:
        def sb(name, shape, dt=F32):
            return ctx.enter_context(nc.sbuf_tensor(name, shape, dt))

        def psum(name, shape, dt=F32):
            return ctx.enter_context(nc.psum_tensor(name, shape, dt))

        def sem(name):
            return ctx.enter_context(nc.semaphore(name))

        expert_in = nc.dram_tensor("expert_in", [E * EROWS, D], F32, kind="Internal").ap()
        expert_out = nc.dram_tensor("expert_out", [MT * P, D], F32, kind="Internal").ap()

        res = sb("res", [P, NT, D])
        mem = sb("mem", [P, 2, SC, D + 1])
        memT = sb("memT", [P, 2, DC, S])
        work = sb("work", [P, 5, S])
        score, rest, prob = work[:, 0:2, :], work[:, 2:4, :], work[:, 4, :]
        probT = sb("probT", [P, SC, P])
        qT = sb("qT", [P, DC, T])
        xnT = sb("xnT", [P, DC, T])
        xn = sb("xn", [P, TPB, D])
        xn2 = sb("xn2", [P, 2, TPB, D])
        xn2T = sb("xn2T", [P, DC, T])
        hid = sb("hid", [P, FC, T])
        logitT = hid[0:E, 0, :]
        att = sb("att", [P, 2, D + 1])
        attT = sb("attT", [P, DC, P])
        best = sb("best", [P, 2, 8 * ROUNDS])
        negmax = sb("negmax", [P, 2])
        rowc = sb("rowc", [P, 2, TPB])
        rsum = sb("rsum", [P, 2])
        stats = sb("stats", [P, TPB, 6])
        meanvar = sb("meanvar", [P, TPB, 2])
        rstd = sb("rstd", [P, TPB])
        stats2 = sb("stats2", [P, TPB, 6])
        meanvar2 = sb("meanvar2", [P, TPB, 2])
        rstd2 = sb("rstd2", [P, TPB])
        norm2 = sb("norm2", [P, NT, 2])
        eps = sb("eps", [P, TPB])
        minus_half = sb("minus_half", [P, TPB])
        zeros = sb("zeros", [P, TPB])
        ident = sb("ident", [P, P])
        before = sb("before", [P, P])
        ones = sb("ones", [P, P])
        iotaE = sb("iotaE", [P, E])
        ebase = sb("ebase", [P, E])
        Sgu_sb = sb("Sgu_sb", [P, DC, 2 * FS])
        Sd_sb = sb("Sd_sb", [P, FC, D])
        Wr_sb = sb("Wr_sb", [P, DC, E])
        Aqk = sb("Aqk", [P, DC, D])
        Cvo = sb("Cvo", [P, DC, D])
        bcols = sb("bcols", [P, 3, DC])
        a_bias = sb("a_bias", [P, DC])
        w_row = sb("w_row", [P, D])
        rowsum = sb("rowsum", [P, TPB])
        rowc0 = sb("rowc0", [P, 1])
        out_bias = sb("out_bias", [P, D])
        logit = sb("logit", [P, TPB, E])
        lneg = sb("lneg", [P, TPB])
        rexp = sb("rexp", [P, TPB, E])
        rexps = sb("rexps", [P, TPB])
        rinv = sb("rinv", [P, TPB])
        rtop = sb("rtop", [P, TPB, 8])
        ridx = sb("ridx", [P, TPB, 8], U32)
        chosen = logit
        cum = sb("cum", [P, TPB + 1, E])
        rank = rexp
        onehot = sb("onehot", [P, TPB, 2, E])
        choice = sb("choice", [P, TPB, 2])
        slot = sb("slot", [P, NT, 2])
        gates = sb("gates", [P, NT, 2])
        slot_i = sb("slot_i", [P, 2, TPB, 2], I32)
        tiles_i = sb("tiles_i", [P, E], I32)
        gidx = sb("gidx", [P, 2, TPB, 2], I32)
        pad_row = sb("pad_row", [P, E], I32)

        def weight(buf, i, w):
            return buf[:, i, w * DC * D:(w + 1) * DC * D].rearrange("p (c n) -> p c n", c=DC)

        Wq_sb, Wk_sb, Wv_sb, Wo_sb = weight(work, 2, 0), weight(work, 2, 1), weight(work, 2, 2), weight(work, 3, 0)
        WoT_sb = weight(work, 4, 0)
        brows, bo_row = work[0:3 * DC, 0, 0:P], work[0:1, 1, 0:D]
        bq_wide, bk_wide, bv_wide = (work[:, 4, (2 + i) * DC * P + D:(3 + i) * DC * P + D].rearrange("p (c n) -> p c n", c=DC)
                                     for i in range(3))

        scoreP = psum("scoreP", [P, 2048])
        turnP = [psum(f"turnP{i}", [P, 512]) for i in range(2)]
        pvP = psum("pvP", [P, 512])
        outP = psum("outP", [P, 512])

        SETUP_COPIES = 7
        NWEIGHTS = 16 * 3
        LATE_LOADS = 2 * 2 * DC + 2
        PADS_PLANNED = 3
        TILES_MADE = PADS_PLANNED + 3 + 2 * 4 + 8
        TILES_PLANNED = TILES_MADE + 2
        PLAN = TILES_PLANNED + 8

        flat_mem, flat_memT, flat_work = (mem[:].rearrange("p a c d -> p (a c d)"), memT[:].rearrange("p a c s -> p (a c s)"),
                                          work[:].rearrange("p a s -> p (a s)"))
        at = [0]

        def reuse(of, n):
            at[0] += n
            assert at[0] <= of.shape[1]
            return of[:, at[0] - n:at[0]]

        assert E // 2 * 2 * F <= SC * (D + 1) and E // 2 * D <= DC * S
        Wgu1_sb = reuse(flat_mem, E * 2 * F).rearrange("p (e f) -> p e f", e=E)
        xin = reuse(flat_mem, RING * D).rearrange("p (r d) -> p r d", r=RING)
        zero_rows = reuse(flat_mem, D)
        at[0] = 0
        xn3T = reuse(flat_mem, 2 * DC * T).rearrange("p (q c t) -> p q c t", q=2, c=DC)
        tanh3 = reuse(flat_mem, 2 * T).rearrange("p (h t) -> p h t", h=2)
        at[0] = 0
        Wd_sb = reuse(flat_memT, E * D).rearrange("p (e d) -> p e d", e=E)
        passed = reuse(flat_memT, TC * E).rearrange("p (t e) -> p t e", e=E)
        at[0] = 0
        Wgu0_sb = reuse(flat_work, E * 2 * F).rearrange("p (e f) -> p e f", e=E)
        shifted = reuse(flat_work, 2 * NT * E).rearrange("p (t e) -> p t e", e=E)
        count, tiles, incl0, incl1, excl, shift, shift_step, gap, padf = (reuse(flat_work, E) for _ in range(9))
        lastt, yrow, tidx, gone_rows = (reuse(flat_work, n) for n in (1, 2 * NT, TC, TC))
        tile_plan = reuse(flat_work, 2 * TC).rearrange("p (k c) -> p k c", k=2)
        at[0] = 0
        gath = reuse(flat_work, 2 * TPB * 2 * D).rearrange("p (r k d) -> p r k d", r=2 * TPB, k=2)
        at[0] = E * 2 * F
        yout = reuse(flat_work, RING // 2 * D).rearrange("p (r d) -> p r d", r=RING // 2)
        incl = [incl0, incl1]
        Wgu_sb = [Wgu0_sb, Wgu1_sb]
        xinT = qT[:].rearrange("p c t -> p (c t)")[:, 0:2 * D].rearrange("p (q c n) -> p q c n", q=2, c=DC)
        etanh, ehid, ehidT = (xnT[:, 0, 0:2 * P].rearrange("p (q n) -> p q n", q=2),
                              xnT[:, 0, 2 * P:4 * P].rearrange("p (q n) -> p q n", q=2),
                              xnT[:, 1, 0:2 * P].rearrange("p (q n) -> p q n", q=2))
        flat_probT = probT[:].rearrange("p c n -> p (c n)")
        at[0] = 0
        iota_t = reuse(flat_probT, TC)
        yrow_i = reuse(flat_probT, 2 * NT).bitcast(I32).rearrange("p (t k) -> p t k", k=2)
        tile_row, tile_expert = (reuse(flat_probT, MT).bitcast(I32) for _ in range(2))
        guP = [scoreP[:, 512 * i:512 * i + 512] for i in range(2)]
        ehTP = [scoreP[:, 512 * i:512 * i + 512] for i in range(2, 4)]
        yP = [pvP, outP]
        sguP = [scoreP[:, 512 * i:512 * i + 512] for i in range(2 * FC)]

        s_small = sem("small_loaded")
        s_weights = sem("ffn_weights_loaded")
        s_x = sem("x_loaded")
        s_late = sem("late_weights_loaded")
        s_mem = [sem(f"mem_loaded{i}") for i in range(2)]
        s_const = sem("constants_made")
        s_wide = sem("wide_biases")
        s_bcol = sem("bias_columns")
        s_setup_p = sem("setup_product")
        s_setup_c = sem("setup_copied")
        s_scored = sem("scores_in_psum")
        s_score = sem("scores_copied")
        s_topk = sem("topk_step")
        s_neg = sem("negmax_ready")
        s_exp = sem("exps_done")
        s_masked = sem("prob_masked")
        s_turn = sem("turned")
        s_turnread = sem("turn_read")
        s_pv = sem("pv_done")
        s_att = sem("att_copied")
        s_proj = sem("proj_done")
        s_rsum = sem("rsum_ready")
        s_res = sem("residual_added")
        s_ln = sem("ln1_stats")
        s_lnp = sem("ln1_rstd")
        s_xn = sem("xn_ready")
        s_xnT = sem("xnT_copied")
        s_xnw = sem("xn_times_w")
        s_rowc = sem("row_constant_step")
        s_bias = sem("bias_added")
        s_ln2 = sem("ln2_stats")
        s_ln2p = sem("ln2_rstd")
        s_xn2 = sem("xn2_ready")
        s_logit = sem("logits_copied")
        s_rankc = sem("ranks_copied")
        s_route = sem("route_step")
        s_rexp = sem("route_exp")
        s_cum = sem("cum_step")
        s_scat = [sem(f"rows_scattered{i}") for i in range(2)]
        s_held = {k: sem(f"held_{k}") for k in ("pool", "dve", "pe")}
        s_count = sem("counts_summed")
        s_plan = sem("plan_step")
        s_iota = sem("tile_numbers_made")
        s_tiles = sem("tile_plan_turned")
        s_zero = sem("zero_rows_made")
        s_pad = [sem(f"pad_rows_written{i}") for i in range(2)]
        s_ein = [sem(f"expert_rows_loaded{i}") for i in range(RING)]
        s_eturn = sem("expert_rows_turned")
        s_eturnc = sem("expert_rows_copied")
        s_gu = sem("gate_up_done")
        s_eact = sem("expert_tanh")
        s_eh = sem("expert_hidden_step")
        s_ehT = sem("expert_hidden_turned")
        s_ehTc = sem("expert_hiddenT_copied")
        s_ydone = sem("expert_out_product")
        s_y = sem("expert_out_copied")
        s_ystore = [sem(f"expert_out_stored{i}") for i in range(RING)]
        s_xn3 = sem("xn3_ready")
        s_turn3 = sem("xn3_turned")
        s_turn3c = sem("xn3T_copied")
        s_sgu = sem("shared_gate_up_done")
        s_sact = sem("shared_tanh")
        s_hid = sem("shared_hidden_step")
        s_sdown = sem("shared_down_done")
        s_shared = sem("shared_added")
        s_gidx = sem("gather_rows_ready")
        s_gath = [sem(f"rows_gathered{i}") for i in range(2 * TPB)]
        s_final = sem("final_step")
        s_out = sem("out_stored")

        block = ctx.enter_context(nc.Block())

        PAIR = 2 * TPB
        NP = B // 2

        def walk(eng, step, turn=None):
            for t in range(PAIR):
                step(t, t // TPB, t % TPB, t // TPB % 2)
            if turn:
                first, per = turn.n, 2 * BATCH_TURNS
                odd = first % 2
            with eng.Fori(1, NP - 1) as p:
                if turn:
                    turn.at(p * per + (first - odd - per), odd)
                for j in range(PAIR):
                    step(p * PAIR + j, p * 2 + j // TPB, j % TPB, j // TPB)
                assert turn is None or turn.n == per + odd
            if turn:
                turn.at((NP - 2) * per + first - odd, odd)
            for t in range(NT - PAIR, NT + 2 * TPB):
                step(t, t // TPB, t % TPB, t // TPB % 2)

        def ewalk(eng, step):
            for i in range(BODY):
                step(i, i)
            with eng.Fori(1, MT // BODY) as p:
                for r in range(BODY):
                    step(p * BODY + r, r)
            for i in range(MT, MT + 6):
                step(i, i % BODY)

        def swalk(eng, step):
            for b in range(2):
                step(b, b)
            with eng.Fori(0, (B - 4) // 4) as p:
                for i in range(4):
                    step(p * 4 + (i + 2), i % 2)
            for b in range(B - 2, B + 1):
                step(b, b % 2)

        def zero_pads(eng, half):
            eng.wait_ge(s_zero, 1)
            eng.wait_ge(s_plan, PADS_PLANNED)
            for e0 in range(half * E // 2, (half + 1) * E // 2, 4):
                firsts = [eng.value_load(pad_row[0:1, e:e + 1], min_val=0, max_val=(E - 1) * EROWS + B * T)
                          for e in range(e0, e0 + 4)]
                for row in firsts:
                    eng.dma_start(expert_in[bass.ds(row, P), :], zero_rows).then_inc(s_pad[half], 16)

        @block.sync
        def _(sp):
            def load_x(b):
                sp.dma_start(res[:, bass.ds(b * TPB, TPB), :], x_t[:, bass.ds(b * TPB, TPB), :]).then_inc(s_x, 16)

            def load_mem(b, par):
                src = ctx_1024[bass.ds(b, 1), :, :]
                sp.dma_start(mem[:, par, 0:SF, 0:D],
                             src[:, 0:SF * P, :].rearrange("a (c p) d -> p (a c) d", p=P)).then_inc(s_mem[par], 16)
                sp.dma_start(mem[0:SR, par, SF, 0:D],
                             src[:, SF * P:S, :].rearrange("a p d -> p (a d)")).then_inc(s_mem[par], 16)

            load_x(0)
            for w_sb, w in ((Wq_sb, Wq), (Wk_sb, Wk), (Wv_sb, Wv), (Wo_sb, Wo)):
                sp.dma_start(w_sb, w.rearrange("(c p) n -> p c n", p=P)).then_inc(s_small, 16)
            for n, bias in enumerate((bq, bk, bv)):
                sp.dma_start(brows[n * DC:(n + 1) * DC, :], bias.rearrange("(c p) -> c p", p=P)).then_inc(s_small, 16)
            sp.dma_start(bo_row[:, :], bo.rearrange("(a n) -> a n", a=1)).then_inc(s_small, 16)
            load_mem(0, 0)
            sp.wait_ge(s_x, 16)
            load_x(1)
            load_mem(1, 1)
            sp.dma_start(Sgu_sb[:, :, 0:FS], Sg.rearrange("(c p) f -> p c f", p=P)).then_inc(s_weights, 16)
            sp.dma_start(Sgu_sb[:, :, FS:2 * FS], Su.rearrange("(c p) f -> p c f", p=P)).then_inc(s_weights, 16)
            sp.dma_start(Sd_sb[:], Sd.rearrange("(c p) d -> p c d", p=P)).then_inc(s_weights, 16)

            def load_gate_up(c, e):
                for w, src in enumerate((Wg, Wu)):
                    sp.dma_start(Wgu_sb[c][:, e:e + E // 2, w * F:(w + 1) * F],
                                 src[e:e + E // 2, c * P:(c + 1) * P, :].rearrange("e p f -> p e f")).then_inc(s_late, 16)

            def load_down(e):
                sp.dma_start(Wd_sb[:, e:e + E // 2, :], Wd[e:e + E // 2].rearrange("e p d -> p e d")).then_inc(s_late, 16)

            with sp.Fori(1, NP) as p:
                for par in range(2):
                    b = p * 2 + par
                    sp.wait_ge(s_x, b * 16)
                    load_x(b)
                    sp.wait_ge(s_pv, b * TPB - TPB)
                    load_mem(b, par)

            sp.wait_ge(s_scored, 2 * (NT - TPB))
            sp.wait_ge(s_pv, NT - TPB)
            load_gate_up(1, 0)
            load_down(0)
            sp.wait_ge(s_scored, 2 * NT)
            sp.wait_ge(s_pv, NT)
            load_gate_up(1, E // 2)
            load_down(E // 2)
            load_gate_up(0, 0)
            load_gate_up(0, E // 2)

            zero_pads(sp, 0)
            for q in range(2):
                sp.wait_ge(s_scat[q], NP * TPB * 2 * 16 + 16)
            for half in range(2):
                sp.wait_ge(s_pad[half], E // 2 * 16)
            sp.wait_ge(s_plan, TILES_PLANNED)

            def load_rows(i, r):
                row = sp.value_load(tile_row[0:1, bass.ds(i, 1)], min_val=0, max_val=(E - 1) * EROWS + B * T)
                sp.dma_start(xin[:, r, :], expert_in[bass.ds(row, P), :]).then_inc(s_ein[r], 16)

            for i in range(RING):
                load_rows(i, i)
            with sp.Fori(1, MT // RING) as p:
                for r in range(RING):
                    sp.wait_ge(s_eturn, p * RING + (r + 1 - RING))
                    load_rows(p * RING + r, r)
            with sp.Fori(0, B - 1) as p:
                sp.wait_ge(s_final, p * (2 * TPB) + 2 * TPB)
                sp.dma_start(out_t[:, bass.ds(p * TPB, TPB), :], res[:, bass.ds(p * TPB, TPB), :]).then_inc(s_out, 16)
            for tile in range(NT - TPB, NT):
                sp.wait_ge(s_final, 2 * tile + 2)
                sp.dma_start(out_t[:, tile:tile + 1, :], res[:, tile:tile + 1, :]).then_inc(s_out, 16)
            sp.wait_ge(s_out, (B - 1 + TPB) * 16)

        @block.gpsimd
        def _(pool):
            nc.gpsimd.memset(ident[:], 0.0).then_inc(s_const, 1)
            nc.gpsimd.memset(ones[:], 1.0).then_inc(s_const, 1)
            nc.gpsimd.memset(eps[:], LN_EPS).then_inc(s_const, 1)
            nc.gpsimd.memset(minus_half[:], -0.5).then_inc(s_const, 1)
            nc.gpsimd.memset(zeros[:], 0.0).then_inc(s_const, 1)
            nc.gpsimd.memset(cum[:], 0.0).then_inc(s_cum, 1)
            nc.gpsimd.memset(mem[:, :, :, D:D + 1], 1.0).then_inc(s_const, 1)
            nc.gpsimd.iota(iotaE[:], pattern=[[1, E]], base=0, channel_multiplier=0,
                           allow_small_or_imprecise_dtypes=True).then_inc(s_const, 1)
            nc.gpsimd.iota(ebase[:], pattern=[[EROWS, E]], base=0, channel_multiplier=0,
                           allow_small_or_imprecise_dtypes=True).then_inc(s_const, 1)
            for c in range(DC):
                nc.gpsimd.dma_start(Wr_sb[:, c, :], Wr[c * P:(c + 1) * P, :]).then_inc(s_scat[c], 16)
            pool.wait_ge(s_const, 8)
            nc.gpsimd.affine_select(out=ident[:], in_=ident[:], compare_op=ALU.not_equal, fill=1.0, base=0,
                                    pattern=[[-1, P]], channel_multiplier=1).then_inc(s_const, 1)
            nc.gpsimd.affine_select(out=before[:], in_=ones[:], compare_op=ALU.is_ge, fill=0.0, base=-1,
                                    pattern=[[1, P]], channel_multiplier=-1).then_inc(s_const, 1)

            def rstd_of(mv, to, stats_sem, n, done, k):
                pool.wait_ge(stats_sem, n)
                nc.gpsimd.tensor_tensor(to[:], mv[:, :, 1], eps[:], ALU.add).then_inc(done, 1)
                pool.wait_ge(done, k)
                nc.gpsimd.tensor_tensor(to[:], to[:], minus_half[:], ALU.pow).then_inc(done, 1)

            def add_bias(b):
                pool.wait_ge(s_xn, b * TPB + TPB)
                rb = res[:, bass.ds(b * TPB, TPB), :]
                nc.gpsimd.tensor_tensor(rb, rb, out_bias[:, None, :].to_broadcast([P, TPB, D]), ALU.add).then_inc(s_bias, 1)

            def row_constants(b, q):
                pool.wait_ge(s_xnT, b + 1)
                nc.gpsimd.tensor_tensor(xn[:], xn[:], w_row[:, None, :].to_broadcast([P, TPB, D]), ALU.mult).then_inc(s_xnw, 1)
                w, n = D // 2, 1
                while w > 1:
                    pool.wait_ge(s_xnw, b * HALVINGS + n)
                    nc.gpsimd.tensor_tensor(xn[:, :, 0:w], xn[:, :, 0:w], xn[:, :, w:2 * w], ALU.add).then_inc(s_xnw, 1)
                    w, n = w // 2, n + 1
                assert n == HALVINGS
                pool.wait_ge(s_xnw, b * HALVINGS + n)
                if since(b, 2):
                    pool.wait_ge(s_score, b * (2 * TPB) - 2 * TPB)
                nc.gpsimd.tensor_tensor(rowsum[:], xn[:, :, 0], xn[:, :, 1], ALU.add).then_inc(s_rowc, 1)
                pool.wait_ge(s_rowc, b * 2 + 1)
                pool.sem_inc(s_held["pool"], 1)
                nc.gpsimd.tensor_scalar(rowc[:, q, :], rowsum[:], SCALE, rowc0[:, 0:1], ALU.mult, ALU.add).then_inc(s_rowc, 1)

            rstd_of(meanvar, rstd, s_ln, 2 * TPB, s_lnp, 1)
            pool.wait_ge(s_setup_c, SETUP_COPIES)
            add_bias(0)
            row_constants(0, 0)

            def step(t, b, j, par):
                if live(t, 2, NT):
                    pool.wait_ge(s_exp, t * 2 - 2)
                    for a, z in ((0, HALF), (HALF, S)):
                        nc.gpsimd.tensor_tensor(prob[:, a:z], prob[:, a:z], rest[:, j % 2, a:z], ALU.subtract).then_inc(s_masked, 1)
                if isinstance(b, int) and b == B + 1 and j == 0:
                    pool.wait_ge(s_pv, NT)
                    nc.gpsimd.iota(iota_t, pattern=[[P, TC]], base=0, channel_multiplier=1,
                                   allow_small_or_imprecise_dtypes=True).then_inc(s_iota, 1)
                if j == 1 and live(b, -1, B):
                    rstd_of(meanvar, rstd, s_ln, b * 8 + 16, s_lnp, b * 2 + 3)
                if j == 2 and live(b, 2, B):
                    pool.wait_ge(s_route, b * RK - 2 * RK + 15)
                    for n in range(TPB):
                        pool.wait_ge(s_cum, b * 5 - 9 + n)
                        nc.gpsimd.tensor_tensor(cum[:, n + 1, :], cum[:, n, :], chosen[:, n, :], ALU.add).then_inc(s_cum, 1)
                if j == 2 and live(b, -1, B):
                    add_bias(b + 1)
                if j == 3 and live(b, -1, B):
                    row_constants(b + 1, (par + 1) % 2)
                if j == 3 and live(b, 1, B):
                    rstd_of(meanvar2, rstd2, s_ln2, b * 8, s_ln2p, b * 3 - 2)
                    mt = bass.ds(b * TPB - TPB, TPB)
                    nc.gpsimd.tensor_tensor(norm2[:, mt, 0], meanvar2[:, :, 0], zeros[:], ALU.add)
                    pool.wait_ge(s_ln2p, b * 3 - 1)
                    nc.gpsimd.tensor_tensor(norm2[:, mt, 1], rstd2[:], zeros[:], ALU.add).then_inc(s_ln2p, 1)
                if j == 3 and live(b, 2, B):
                    pool.wait_ge(s_cum, b * 5 - 9 + TPB)
                    pool.wait_ge(s_rankc, b - 1)
                    pool.sem_inc(s_held["pool"], 1)
                    nc.gpsimd.tensor_copy(cum[:, 0, :], cum[:, TPB, :]).then_inc(s_cum, 1)
                    pool.wait_ge(s_route, b * RK - RK)
                    pool.sem_inc(s_held["pool"], 1)
                    for n in range(TPB):
                        for k in range(2):
                            nc.gpsimd.indirect_dma_start(
                                out=expert_in[:, :], out_offset=bass.IndirectOffsetOnAxis(ap=slot_i[:, par, n, k:k + 1], axis=0),
                                in_=xn2[:, par, n, :], in_offset=None).then_inc(s_scat[par], 16)

            walk(pool, step)

            for r in range(RING):
                pool.wait_ge(s_ystore[r], MT // RING * 16)
            with pool.Fori(0, NT // (2 * TPB)) as p:
                for h in range(2):
                    pool.wait_ge(s_gidx, p * 2 + h + 1)
                    pool.sem_inc(s_held["pool"], 1)
                    for r in range(TPB):
                        for k in range(2):
                            nc.gpsimd.indirect_dma_start(
                                out=gath[:, h * TPB + r, k, :], out_offset=None, in_=expert_out[:, :],
                                in_offset=bass.IndirectOffsetOnAxis(ap=gidx[:, h, r, k:k + 1], axis=0)).then_inc(s_gath[h * TPB + r], 16)

        @block.scalar
        def _(act):
            turn = Count()

            def take():
                act.wait_ge(s_turn, turn.next())
                return turnP[(turn.n - 1) % 2]

            def signal(to):
                act.wait_ge(s_turnread, turn.now())
                act.sem_inc(to, 1)

            act.wait_ge(s_bcol, 1)
            nc.scalar.activation(bcols[:].rearrange("p n c -> p (n c)"), outP[:, 0:3 * DC], ACT.Copy).then_inc(s_bcol, 1)
            act.wait_ge(s_setup_p, 1)
            nc.scalar.activation(WoT_sb, turnP[0][:].rearrange("p (c n) -> p c n", c=DC), ACT.Copy).then_inc(s_setup_c, 1)
            act.wait_ge(s_setup_p, 2)
            nc.scalar.activation(Aqk[:], turnP[1][:].rearrange("p (c n) -> p c n", c=DC), ACT.Copy).then_inc(s_setup_c, 1)
            act.wait_ge(s_setup_p, 3)
            nc.scalar.activation(a_bias[:], pvP[:, 0:DC], ACT.Copy, scale=SCALE).then_inc(s_setup_c, 1)
            nc.scalar.activation(rowc0[:], pvP[:, 16:17], ACT.Copy, scale=SCALE).then_inc(s_setup_c, 1)
            act.wait_ge(s_setup_p, 4)
            nc.scalar.activation(Cvo[:], turnP[0][:].rearrange("p (c n) -> p c n", c=DC), ACT.Copy).then_inc(s_setup_c, 1)
            act.wait_ge(s_setup_p, 5)
            nc.scalar.activation(out_bias[:], outP[:, 0:D], ACT.Copy).then_inc(s_setup_c, 1)
            nc.scalar.activation(w_row[:], outP[:, D:2 * D], ACT.Copy).then_inc(s_setup_c, 1)

            def copy_memT(q, i):
                h, g = i % DC, GROUPS[i // DC]
                w = sum(rows(c) for c in g)
                src = take()
                nc.scalar.activation(memT[:, q, h, g[0] * P:g[0] * P + w], src[:, 0:w], ACT.Copy).then_inc(s_turnread, 1)

            def copy_xnT(c):
                src = take()
                nc.scalar.activation(xnT[:, c, :], src[:], ACT.Copy).then_inc(s_turnread, 1)
                if c == DC - 1:
                    signal(s_xnT)

            def copy_qT(c):
                src = take()
                nc.scalar.activation(qT[:, c, :], src[:], ACT.Identity, scale=SCALE,
                                     bias=a_bias[:, c:c + 1]).then_inc(s_turnread, 1)

            act.wait_ge(s_setup_c, SETUP_COPIES)
            for c in range(DC):
                copy_xnT(c)
            for c in range(DC):
                copy_qT(c)
            for i in range(MEM_TURNS):
                copy_memT(0, i)

            def step(t, b, j, par):
                if live(t, 2, NT):
                    act.wait_ge(s_topk, t * TK - TK)
                    nc.scalar.activation(rest[:, j % 2, :], rest[:, j % 2, :], ACT.Exp, bias=negmax[:, j % 2:j % 2 + 1]).then_inc(s_exp, 1)
                if live(t, 0, NT):
                    if j == 0:
                        act.wait_ge(s_rowc, b * 2 + 2)
                    act.wait_ge(s_scored, t * 2 + 1)
                    if since(t, 2):
                        act.wait_ge(s_topk, t * TK - 2 * TK + 2)
                        act.wait_ge(s_exp, t * 2 - 3)
                    nc.scalar.activation(score[:, j % 2, 0:HALF], scoreP[:, 0:HALF], ACT.Identity,
                                         bias=rowc[:, par, j:j + 1]).then_inc(s_score, 1)
                    act.wait_ge(s_scored, t * 2 + 2)
                    nc.scalar.activation(score[:, j % 2, HALF:S], scoreP[:, HALF:S], ACT.Identity,
                                         bias=rowc[:, par, j:j + 1]).then_inc(s_score, 1)
                if live(t, 3, NT):
                    src = take()
                    if since(t, 4):
                        act.wait_ge(s_proj, t - 3)
                    nc.scalar.activation(attT[:], src[:, 0:D].rearrange("p (c n) -> p c n", c=DC), ACT.Copy).then_inc(s_turnread, 1)

                def beside(i):
                    if j == 0 and live(b, 2, B):
                        src = take()
                        if i < DC:
                            nc.scalar.activation(xn2T[:, i, :], src[:], ACT.Copy).then_inc(s_turnread, 1)
                        if i == 2:
                            nc.scalar.activation(logitT, src[0:E, :], ACT.Copy).then_inc(s_turnread, 1)
                        if i == 3:
                            nc.scalar.activation(logit[:], src[:, 0:TPB * E].rearrange("p (j e) -> p j e", e=E),
                                                 ACT.Copy).then_inc(s_turnread, 1)
                            signal(s_logit)
                    if j == 2 and i in (1, 2) and live(b, -1, B):
                        copy_xnT(i - 1)
                    if j == 3 and live(b, -1, B):
                        if i < DC:
                            copy_qT(i)
                        for m in MEM_BESIDE[i]:
                            copy_memT((par + 1) % 2, m)

                def copy_probT(g):
                    if live(t, 2, NT):
                        src = take()
                        if g[0] == 0 and since(t, 3):
                            act.wait_ge(s_pv, t - 2)
                        r = rows(g[-1])
                        nc.scalar.activation(probT[0:r, g[0]:g[-1] + 1, :],
                                             src[0:r, 0:len(g) * P].rearrange("p (c n) -> p c n", n=P),
                                             ACT.Copy).then_inc(s_turnread, 1)

                for g in GROUPS[:2]:
                    copy_probT(g)
                for i in range(NG - 1):
                    if i + 2 < NG:
                        copy_probT(GROUPS[i + 2])
                    beside(i)
                if j != 3 and live(t, 1, NT):
                    act.wait_ge(s_neg, t)
                    q = (j - 1) % 2
                    nc.scalar.activation(prob, score[:, q, :], ACT.Exp, bias=negmax[:, q:q + 1]).then_inc(s_exp, 1)
                if j == 1 and live(b, 2, B):
                    act.wait_ge(s_route, b * RK - 2 * RK + 2)
                    for n in range(TPB):
                        nc.scalar.activation(rexp[:, n, :], logit[:, n, :], ACT.Exp, bias=lneg[:, n:n + 1],
                                             accum_out=rexps[:, n:n + 1]).then_inc(s_rexp, 1)
                beside(NG - 1)
                if live(t, 2, NT):
                    act.wait_ge(s_pv, t - 1)
                    if since(t, 4):
                        act.wait_ge(s_proj, t - 3)
                        act.wait_ge(s_rsum, t - 3)
                    nc.scalar.activation(att[:, j % 2, :], pvP[:, 0:D + 1], ACT.Copy).then_inc(s_att, 1)
                if j == 2 and live(b, 2, B):
                    src = take()
                    nc.scalar.activation(rank[:], src[:, 0:TPB * E].rearrange("p (j e) -> p j e", e=E),
                                         ACT.Copy).then_inc(s_turnread, 1)
                    signal(s_rankc)
                if j == 3 and live(b, -1, B):
                    for m in MEM_LATE:
                        copy_memT((par + 1) % 2, m)

                if j == 3 and live(t, 1, NT):
                    act.wait_ge(s_neg, t)
                    q = (j - 1) % 2
                    nc.scalar.activation(prob, score[:, q, :], ACT.Exp, bias=negmax[:, q:q + 1]).then_inc(s_exp, 1)

            walk(act, step, turn)
            zero_pads(act, 1)

            def estep(i, r):
                if live(i, 2, MT):
                    q = r % 2
                    act.wait_ge(s_gu, i - 1)
                    if since(i, 4):
                        act.wait_ge(s_eh, i * 2 - 6)
                    nc.scalar.activation(etanh[:, q, :], guP[q][:, 0:F], ACT.Tanh, scale=0.5).then_inc(s_eact, 1)
                if live(i, 0, MT):
                    act.wait_ge(s_eturn, i + 1)
                    nc.scalar.activation(xinT[:, r % 2], turnP[r % 2][:, 0:D].rearrange("p (c n) -> p c n", c=DC),
                                         ACT.Copy).then_inc(s_eturnc, 1)
                if live(i, 5, MT):
                    q = (r - 5) % RING
                    act.wait_ge(s_y, i - 4)
                    act.dma_start(expert_out[bass.ds(i * P - 5 * P, P), :], yout[:, q % (RING // 2), :]).then_inc(s_ystore[q], 16)
                if live(i, 4, MT):
                    q = (r - 4) % RING
                    act.wait_ge(s_ydone, i - 3)
                    if since(i, RING // 2 + 4):
                        h = (q + RING // 2) % RING
                        act.wait_ge(s_ystore[h], (i - 4 - RING // 2 - h) * 2 + 16)
                    nc.scalar.activation(yout[:, q % (RING // 2), :], yP[q % 2][:, 0:D], ACT.Copy).then_inc(s_y, 1)

            ewalk(act, estep)

            act.wait_ge(s_ydone, MT)

            def copy_xn3T(b, q):
                for c in range(DC):
                    act.wait_ge(s_turn3, b * DC + c + 1)
                    if c == 0 and since(b, 2):
                        act.wait_ge(s_sgu, b * 2 - 2)
                    nc.scalar.activation(xn3T[:, q, c, :], turnP[c][:], ACT.Copy).then_inc(s_turn3c, 1)

            def tanh_half(b, h):
                act.wait_ge(s_sgu, b * 2 + h + 1)
                if since(b, 1):
                    act.wait_ge(s_hid, b * 4 + 2 * h - 3)
                nc.scalar.activation(tanh3[:, h, :], sguP[2 * h], ACT.Tanh, scale=0.5).then_inc(s_sact, 1)

            def sstep(b, q):
                if live(b, 0, B):
                    tanh_half(b, 0)
                if live(b, -1, B):
                    copy_xn3T(b + 1, (q + 1) % 2)
                if live(b, 0, B):
                    tanh_half(b, 1)

            copy_xn3T(0, 0)
            swalk(act, sstep)

        @block.vector
        def _(dve):
            def stats1(b, half):
                if half == 0:
                    dve.wait_ge(s_x, b * 16 + 16)
                    if since(b, 1):
                        dve.wait_ge(s_xn, b * TPB)
                    dve.sem_inc(s_held["dve"], 1)
                for n in range(2 * half, 2 * half + 2):
                    nc.vector.bn_stats(stats[:, n, :], res[:, b * TPB + n, :]).then_inc(s_ln, 1)

            def meanvar1(b):
                dve.wait_ge(s_ln, b * 8 + TPB)
                dve.sem_inc(s_held["dve"], 1)
                for n in range(TPB):
                    nc.vector.bn_aggr(meanvar[:, n, :], stats[:, n, :]).then_inc(s_ln, 1)

            def normed1(b, half):
                if half == 0:
                    dve.wait_ge(s_lnp, b * 2 + 2)
                    if since(b, 1):
                        dve.wait_ge(s_rowc, b * 2)
                for n in range(2 * half, 2 * half + 2):
                    nc.vector.tensor_scalar(xn[:, n, :], res[:, b * TPB + n, :], meanvar[:, n, 0:1], rstd[:, n:n + 1],
                                            ALU.subtract, ALU.mult).then_inc(s_xn, 1)

            dve.wait_ge(s_const, 10)
            dve.wait_ge(s_bcol, 2)
            for c in range(DC):
                nc.vector.tensor_scalar(bq_wide[:, c, :], ones[:], bcols[:, 0, c:c + 1], None, ALU.mult).then_inc(s_wide, 1)
                nc.vector.tensor_scalar(bk_wide[:, c, :], ones[:], bcols[:, 1, c:c + 1], None, ALU.mult).then_inc(s_wide, 1)
                nc.vector.tensor_scalar(bv_wide[:, c, :], ones[:], bcols[:, 2, c:c + 1], None, ALU.mult).then_inc(s_wide, 1)
            for half in range(2):
                stats1(0, half)
            meanvar1(0)
            for half in range(2):
                normed1(0, half)

            def residual(t, j, b, i):
                q, n2 = (j + 1) % 2, (j + 1) % TPB
                r = res[:, t - 3, :]
                if i == 3:
                    dve.wait_ge(s_att, t - 2)
                    if since(t, 5):
                        dve.wait_ge(s_res, t - 4)
                    nc.vector.reciprocal(rsum[:, q:q + 1], att[:, q, D:D + 1]).then_inc(s_rsum, 1)
                if i == 4:
                    dve.wait_ge(s_rsum, t - 2)
                    dve.wait_ge(s_proj, t - 2)
                    if j == 3:
                        dve.wait_ge(s_bias, b + 1)
                    nc.vector.scalar_tensor_tensor(out=r, in0=outP[:, 0:D], scalar=rsum[:, q:q + 1], in1=r,
                                                   op0=ALU.mult, op1=ALU.add).then_inc(s_res, 1)
                if i == 5:
                    dve.wait_ge(s_res, t - 2)
                    dve.sem_inc(s_held["dve"], 1)
                    nc.vector.bn_stats(stats2[:, n2, :], r).then_inc(s_ln2, 1)
                if i == 6:
                    dve.wait_ge(s_ln2, t * 2 - 5)
                    if j == 3 and live(b, 1, B):
                        dve.wait_ge(s_xn2, b * TPB)
                    dve.sem_inc(s_held["dve"], 1)
                    nc.vector.bn_aggr(meanvar2[:, n2, :], stats2[:, n2, :]).then_inc(s_ln2, 1)

            def normed2(b, pp, half):
                if half == 0:
                    dve.wait_ge(s_ln2p, b * 3 + 3)
                    if since(b, 2):
                        dve.wait_ge(s_scat[pp], (b - pp) * (TPB * 16) + 16)
                for n in range(2 * half, 2 * half + 2):
                    nc.vector.tensor_scalar(xn2[:, pp, n, :], res[:, b * TPB + n, :],
                                            meanvar2[:, n, 0:1], rstd2[:, n:n + 1],
                                            ALU.subtract, ALU.mult).then_inc(s_xn2, 1)

            def route(b, i):
                r0 = b * RK
                mt = bass.ds(b * TPB, TPB)
                if i == 3:
                    dve.wait_ge(s_rexp, b * TPB + TPB)
                    nc.vector.reciprocal(rinv[:], rexps[:]).then_inc(s_route, 1)
                    dve.sem_inc(s_held["dve"], 1)
                    for n in range(TPB):
                        nc.vector.max(rtop[:, n, :], rexp[:, n, :]).then_inc(s_route, 1)
                if i == 4:
                    dve.wait_ge(s_route, r0 + 7)
                    dve.sem_inc(s_held["dve"], 1)
                    for n in range(TPB):
                        nc.vector.max_index(ridx[:, n, :], rtop[:, n, :], rexp[:, n, :]).then_inc(s_route, 1)
                    nc.vector.tensor_tensor(gates[:, mt, :], rtop[:, :, 0:2], rinv[:, :, None].to_broadcast([P, TPB, 2]),
                                            ALU.mult).then_inc(s_route, 1)
                if i == 5:
                    dve.wait_ge(s_route, r0 + 12)
                    nc.vector.tensor_copy(choice[:], ridx[:, :, 0:2]).then_inc(s_route, 1)
                if i == 6:
                    dve.wait_ge(s_route, r0 + 13)
                    nc.vector.tensor_tensor(onehot[:], iotaE[:, None, None, :].to_broadcast([P, TPB, 2, E]),
                                            choice[:, :, :, None].to_broadcast([P, TPB, 2, E]), ALU.is_equal).then_inc(s_route, 1)
                if i == 7:
                    dve.wait_ge(s_route, r0 + 14)
                    nc.vector.tensor_tensor(chosen[:], onehot[:, :, 0, :], onehot[:, :, 1, :], ALU.add).then_inc(s_route, 1)

            def place(b, par, i):
                r0 = b * RK
                mt = bass.ds(b * TPB, TPB)
                if i == 3:
                    dve.wait_ge(s_rankc, b + 1)
                    nc.vector.tensor_tensor(rank[:], rank[:], ebase[:, None, :].to_broadcast([P, TPB, E]), ALU.add).then_inc(s_route, 1)
                if i == 4:
                    dve.wait_ge(s_route, r0 + 16)
                    nc.vector.tensor_tensor(onehot[:], onehot[:], rank[:, :, None, :].to_broadcast([P, TPB, 2, E]),
                                            ALU.mult).then_inc(s_route, 1)
                if i == 5:
                    dve.wait_ge(s_route, r0 + 17)
                    nc.vector.tensor_reduce(slot[:, mt, :], onehot[:], AX_X, ALU.add).then_inc(s_route, 1)
                if i == 6:
                    dve.wait_ge(s_route, r0 + 18)
                    if since(b, 2):
                        dve.wait_ge(s_scat[par], (b - par) * (TPB * 16) + 16)
                    dve.sem_inc(s_held["dve"], 1)
                    nc.vector.tensor_copy(slot_i[:, par, :, :], slot[:, mt, :]).then_inc(s_route, 1)

            def step(t, b, j, par):
                def beside(i):
                    if j == 3 and live(b, 1, B) and i in (2, 3):
                        normed2(b - 1, (par + 1) % 2, i - 2)
                    if j == 0 and live(b, -1, B):
                        if i < 2:
                            stats1(b + 1, i)
                        if i == 2:
                            meanvar1(b + 1)
                    if j == 1 and live(b, -1, B) and i < 2:
                        normed1(b + 1, i)
                    if j == 0 and live(b, 2, B):
                        if i == 5:
                            dve.wait_ge(s_logit, b - 1)
                            nc.vector.tensor_reduce(lneg[:], logit[:], AX_X, ALU.max).then_inc(s_route, 1)
                        if i == 6:
                            dve.wait_ge(s_route, b * RK - 2 * RK + 1)
                            nc.vector.tensor_scalar(lneg[:], lneg[:], -1.0, None, ALU.mult).then_inc(s_route, 1)
                    if j == 1 and live(b, 2, B):
                        route(b - 2, i)
                    if j == 2 and live(b, 2, B):
                        place(b - 2, par, i)
                    if live(t, 3, NT):
                        residual(t, j, b, i)

                if live(t, 0, NT):
                    q, k0 = j % 2, t * TK
                    dve.wait_ge(s_score, t * 2 + 2)
                    dve.sem_inc(s_held["dve"], 1)
                    nc.vector.max(best[:, q, 0:8], score[:, q, :]).then_inc(s_topk, 1)
                    beside(0)
                    if since(t, 2):
                        dve.wait_ge(s_exp, t * 2 - 2)
                        dve.wait_ge(s_masked, t * 2 - 2)
                    dve.wait_ge(s_topk, k0 + 1)
                    nc.vector.tensor_scalar(negmax[:, q:q + 1], best[:, q, 0:1], -1.0, None, ALU.mult).then_inc(s_neg, 1)
                    nc.vector.match_replace(rest[:, q, :], best[:, q, 0:8], score[:, q, :], GONE).then_inc(s_topk, 1)
                    beside(1)
                    for n in range(1, ROUNDS):
                        b8 = best[:, q, 8 * n:8 * n + 8]
                        dve.wait_ge(s_topk, k0 + 2 * n)
                        dve.sem_inc(s_held["dve"], 1)
                        nc.vector.max(b8, rest[:, q, :]).then_inc(s_topk, 1)
                        beside(2 * n)
                        dve.wait_ge(s_topk, k0 + 2 * n + 1)
                        dve.sem_inc(s_held["dve"], 1)
                        nc.vector.match_replace(rest[:, q, :], b8, rest[:, q, :], GONE).then_inc(s_topk, 1)
                        beside(2 * n + 1)
                else:
                    for i in range(2 * ROUNDS):
                        beside(i)

            walk(dve, step)

            done = Count()

            def then(ins):
                ins.then_inc(s_plan, 1)
                dve.wait_ge(s_plan, done.next())

            dve.wait_ge(s_count, 1)
            dve.wait_ge(s_pv, NT)
            nc.vector.memset(zero_rows, 0.0).then_inc(s_zero, 1)
            then(nc.vector.tensor_copy(count, scoreP[:, 0:E]))
            then(nc.vector.tensor_tensor(padf, count, ebase[:], ALU.add))
            then(nc.vector.tensor_copy(pad_row[:], padf))
            assert done.n == PADS_PLANNED
            then(nc.vector.tensor_scalar(tiles_i[:], count, 1.0 / P, (P - 1.0) / P - 0.5 + 0.5 / P, ALU.mult, ALU.add))
            then(nc.vector.tensor_copy(tiles, tiles_i[:]))
            then(nc.vector.tensor_copy(incl[0], tiles))
            n, a = 1, 0
            while n < E:
                then(nc.vector.tensor_copy(incl[1 - a][:, 0:n], incl[a][:, 0:n]))
                then(nc.vector.tensor_tensor(incl[1 - a][:, n:E], incl[a][:, n:E], incl[a][:, 0:E - n], ALU.add))
                n, a = 2 * n, 1 - a
            upto = incl[a]
            expert_of, row_of = tile_plan[:, 0, :], tile_plan[:, 1, :]
            then(nc.vector.tensor_scalar(lastt, upto[:, E - 1:E], -1.0, None, ALU.add))
            dve.wait_ge(s_iota, 1)
            then(nc.vector.tensor_scalar(tidx, iota_t, lastt, None, ALU.min))
            then(nc.vector.tensor_tensor(passed, tidx[:, :, None].to_broadcast([P, TC, E]),
                                         upto[:, None, :].to_broadcast([P, TC, E]), ALU.is_ge))
            then(nc.vector.tensor_reduce(expert_of, passed, AX_X, ALU.add))
            then(nc.vector.tensor_scalar(gap, tiles, -float(P), float(EROWS), ALU.mult, ALU.add))
            then(nc.vector.tensor_tensor(passed, passed, gap[:, None, :].to_broadcast([P, TC, E]), ALU.mult))
            then(nc.vector.tensor_reduce(gone_rows, passed, AX_X, ALU.add))
            then(nc.vector.scalar_tensor_tensor(out=row_of, in0=tidx, scalar=float(P), in1=gone_rows, op0=ALU.mult, op1=ALU.add))
            assert done.n == TILES_MADE
            dve.wait_ge(s_tiles, 1)
            then(nc.vector.tensor_copy(tile_expert[0:1, :], scoreP[0:1, 512:512 + MT]))
            then(nc.vector.tensor_copy(tile_row[0:1, :], scoreP[0:1, 1024:1024 + MT]))
            assert done.n == TILES_PLANNED
            then(nc.vector.tensor_tensor(excl, upto, tiles, ALU.subtract))
            then(nc.vector.scalar_tensor_tensor(out=shift, in0=excl, scalar=float(P), in1=ebase[:], op0=ALU.mult, op1=ALU.subtract))
            then(nc.vector.tensor_copy(shift_step[:, 0:1], shift[:, 0:1]))
            then(nc.vector.tensor_tensor(shift_step[:, 1:E], shift[:, 1:E], shift[:, 0:E - 1], ALU.subtract))
            then(nc.vector.tensor_tensor(shifted, slot[:].rearrange("p t k -> p (t k)")[:, :, None].to_broadcast([P, 2 * NT, E]),
                                         ebase[:, None, :].to_broadcast([P, 2 * NT, E]), ALU.is_ge))
            then(nc.vector.tensor_tensor(shifted, shifted, shift_step[:, None, :].to_broadcast([P, 2 * NT, E]), ALU.mult))
            then(nc.vector.tensor_reduce(yrow, shifted, AX_X, ALU.add))
            then(nc.vector.tensor_tensor(yrow_i.rearrange("p t k -> p (t k)"), yrow,
                                         slot[:].rearrange("p t k -> p (t k)"), ALU.add))
            assert done.n == PLAN

            def estep(i, r):
                if live(i, 2, MT):
                    q = r % 2
                    g, u = guP[q][:, 0:F], guP[q][:, F:2 * F]
                    dve.wait_ge(s_eact, i - 1)
                    if since(i, 4):
                        dve.wait_ge(s_ehT, i - 3)
                    nc.vector.scalar_tensor_tensor(out=ehid[:, q, :], in0=etanh[:, q, :], scalar=1.0, in1=g,
                                                   op0=ALU.add, op1=ALU.mult).then_inc(s_eh, 1)
                    dve.wait_ge(s_eh, i * 2 - 3)
                    nc.vector.scalar_tensor_tensor(out=ehid[:, q, :], in0=ehid[:, q, :], scalar=0.5, in1=u,
                                                   op0=ALU.mult, op1=ALU.mult).then_inc(s_eh, 1)
                if live(i, 3, MT):
                    q = (r - 3) % 2
                    dve.wait_ge(s_ehT, i - 2)
                    if since(i, 5):
                        dve.wait_ge(s_ydone, i - 4)
                    nc.vector.tensor_copy(ehidT[:, q, :], ehTP[q][:, 0:P]).then_inc(s_ehTc, 1)

            ewalk(dve, estep)

            def norm3(b):
                if since(b, 1):
                    dve.wait_ge(s_turn3, b * DC)
                for n in range(TPB):
                    tile = b * TPB + n
                    nc.vector.tensor_scalar(xn[:, n, :], res[:, tile, :], norm2[:, tile, 0:1], norm2[:, tile, 1:2],
                                            ALU.subtract, ALU.mult).then_inc(s_xn3, 1)

            def hidden(b, h):
                dve.wait_ge(s_sact, b * 2 + h + 1)
                if h == 0 and since(b, 1):
                    dve.wait_ge(s_sdown, b * DC)
                nc.vector.scalar_tensor_tensor(out=hid[:, h, :], in0=tanh3[:, h, :], scalar=1.0, in1=sguP[2 * h],
                                               op0=ALU.add, op1=ALU.mult).then_inc(s_hid, 1)
                dve.wait_ge(s_hid, b * 4 + 2 * h + 1)
                nc.vector.scalar_tensor_tensor(out=hid[:, h, :], in0=hid[:, h, :], scalar=0.5, in1=sguP[2 * h + 1],
                                               op0=ALU.mult, op1=ALU.mult).then_inc(s_hid, 1)

            def add_shared(b):
                for c, bank in enumerate(yP):
                    dve.wait_ge(s_sdown, b * DC + c + 1)
                    rb = res[:, bass.ds(b * TPB + 2 * c, 2), :]
                    nc.vector.tensor_tensor(rb, bank[:].rearrange("p (m d) -> p m d", m=2), rb, ALU.add).then_inc(s_shared, 1)

            def indices(b, h):
                nc.vector.tensor_copy(gidx[:, h, :, :], yrow_i[:, bass.ds(b * TPB, TPB), :]).then_inc(s_gidx, 1)

            def add_up(b, h):
                dve.wait_ge(s_shared, b * DC + DC)
                for r in range(TPB):
                    tile = b * TPB + r
                    rr = res[:, tile, :]
                    dve.wait_ge(s_gath[h * TPB + r], (b - h) * 16 + 32)
                    for k in range(2):
                        if k:
                            dve.wait_ge(s_final, tile * 2 + 1)
                        nc.vector.scalar_tensor_tensor(out=rr, in0=gath[:, h * TPB + r, k, :], scalar=gates[:, tile, k:k + 1], in1=rr,
                                                       op0=ALU.mult, op1=ALU.add).then_inc(s_final, 1)

            def sstep(b, q):
                if live(b, 0, B):
                    hidden(b, 0)
                if live(b, 1, B):
                    add_shared(b - 1)
                if live(b, -2, B):
                    norm3(b + 2)
                if live(b, 0, B):
                    hidden(b, 1)
                if live(b, 1, B):
                    add_up(b - 1, (q + 1) % 2)
                if live(b, 1, B) and live(b, -1, B):
                    dve.wait_ge(s_final, b * (2 * TPB))
                    dve.sem_inc(s_held["dve"], 1)
                    indices(b + 1, (q + 1) % 2)

            for h in range(2):
                indices(h, h)
            dve.wait_ge(s_rowc, B * 2)
            norm3(0)
            norm3(1)
            swalk(dve, sstep)

        @block.tensor
        def _(pe):
            pe.wait_ge(s_const, 10)
            pe.wait_ge(s_small, 16 * 8)
            pe.transpose(outP[:, 0:3 * DC], brows, ident[0:3 * DC, 0:3 * DC]).then_inc(s_bcol, 1)
            for oc in range(DC):
                for c in range(DC):
                    mm = pe.transpose(turnP[0][:, oc * D + c * P:oc * D + (c + 1) * P], Wo_sb[:, c, oc * P:(oc + 1) * P], ident[:])
            mm.then_inc(s_setup_p, 1)

            def product(to, terms):
                for n, (lhsT, rhs) in enumerate(terms):
                    mm = pe.matmul(to, lhsT, rhs, start=(n == 0), stop=(n == len(terms) - 1))
                return mm

            for c in range(DC):
                mm = product(turnP[1][:, c * D:(c + 1) * D], [(Wq_sb[:, o, c * P:(c + 1) * P], Wk_sb[:, o, :]) for o in range(DC)])
            mm.then_inc(s_setup_p, 1)
            pe.wait_ge(s_bcol, 2)
            pe.wait_ge(s_wide, 3 * DC)
            for c in range(DC):
                product(pvP[:, c:c + 1], [(Wk_sb[:, o, c * P:(c + 1) * P], bcols[:, 0, o:o + 1]) for o in range(DC)])
            product(pvP[:, 16:17], [(bq_wide[:, o, :], bcols[:, 1, o:o + 1]) for o in range(DC)]).then_inc(s_setup_p, 1)
            pe.wait_ge(s_setup_c, 1)
            for c in range(DC):
                mm = product(turnP[0][:, c * D:(c + 1) * D], [(Wv_sb[:, o, c * P:(c + 1) * P], WoT_sb[:, o, :]) for o in range(DC)])
            mm.then_inc(s_setup_p, 1)
            product(outP[:, D:2 * D], [(bk_wide[:, o, :], Wq_sb[:, o, :]) for o in range(DC)])
            product(outP[:, 0:D], [(bv_wide[:, o, :], WoT_sb[:, o, :]) for o in range(DC)]
                    + [(ones[0:1, :], bo_row[0:1, :])]).then_inc(s_setup_p, 1)
            pe.wait_ge(s_setup_c, SETUP_COPIES)

            turn = Count()

            def give(after=None):
                n = turn.next()
                if after is not None:
                    pe.wait_ge(s_turnread, after)
                elif not isinstance(n, int) or n > 2:
                    pe.wait_ge(s_turnread, turn.now(2))
                return turnP[(turn.n - 1) % 2]

            def turn_mem(b, q, i):
                h, g = i % DC, GROUPS[i // DC]
                if i == 0:
                    pe.wait_ge(s_mem[q], (b - q) * 16 + 32)
                to = give()
                for n, c in enumerate(g):
                    mm = pe.transpose(to[:, n * P:n * P + rows(c)], mem[0:rows(c), q, c, h * P:(h + 1) * P],
                                      ident[0:rows(c), 0:rows(c)])
                mm.then_inc(s_turn, 1)

            def turn_rows(src, c):
                to = give()
                for n in range(TPB):
                    mm = pe.transpose(to[:, n * P:(n + 1) * P], src(n, c), ident[:])
                mm.then_inc(s_turn, 1)

            def query(c):
                product(give()[:], [(Aqk[:, k, c * P:(c + 1) * P], xnT[:, k, :]) for k in range(DC)]).then_inc(s_turn, 1)

            def xn_part(n, c):
                return xn[:, n, c * P:(c + 1) * P]

            pe.wait_ge(s_xn, TPB)
            for c in range(DC):
                turn_rows(xn_part, c)
            pe.wait_ge(s_turnread, turn.now())
            for c in range(DC):
                query(c)
            for i in range(MEM_TURNS):
                turn_mem(0, 0, i)

            def step(t, b, j, par):
                if live(t, 0, NT):
                    if since(t, 1):
                        pe.wait_ge(s_score, t * 2)
                    for n, (a, z) in enumerate(CHUNKS):
                        if j == 0:
                            pe.wait_ge(s_turnread, turn.now(DC * (NG - 1 - n)))
                        mm = product(scoreP[:, a:z], [(qT[:, k, j * P:(j + 1) * P], memT[:, par, k, a:z]) for k in range(DC)])
                        if z in (HALF, S):
                            mm.then_inc(s_scored, 1)
                if live(t, 3, NT):
                    pe.wait_ge(s_att, t - 2)
                    to = give()
                    attT_copied = turn.now()
                    for c in range(DC):
                        mm = pe.transpose(to[:, c * P:(c + 1) * P], att[:, (j - 3) % 2, c * P:(c + 1) * P], ident[:])
                    mm.then_inc(s_turn, 1)
                def turn_prob(g):
                    to = give()
                    for n, c in enumerate(g):
                        mm = pe.transpose(to[0:rows(c), n * P:(n + 1) * P], prob[:, c * P:c * P + rows(c)], ident[:])
                    mm.then_inc(s_turn, 1)
                    return turn.now()

                def xn2_part(n, c):
                    return xn2[:, par, n, c * P:(c + 1) * P]

                marks = {}

                def beside(i):
                    if j == 0 and live(b, 2, B):
                        if i == 0:
                            pe.wait_ge(s_xn2, b * TPB - TPB)
                        if i < DC:
                            turn_rows(xn2_part, i)
                            marks["xn2T"] = turn.now()
                        if i == 2:
                            if isinstance(b, int) and b == 2 or not isinstance(b, int):
                                for c in range(DC):
                                    pe.wait_ge(s_scat[c], 16)
                            product(give(marks["xn2T"])[0:E, :], [(Wr_sb[:, k, :], xn2T[:, k, :]) for k in range(DC)]).then_inc(s_turn, 1)
                            marks["logitT"] = turn.now()
                        if i == 3:
                            to = give(marks["logitT"])
                            pe.sem_inc(s_held["pe"], 1)
                            for n in range(TPB):
                                mm = pe.transpose(to[:, n * E:(n + 1) * E], logitT[:, n * P:(n + 1) * P], ident[0:E, 0:E])
                            mm.then_inc(s_turn, 1)
                    if j == 2 and i in (1, 2) and live(b, -1, B):
                        if i == 1:
                            pe.wait_ge(s_xn, b * TPB + 2 * TPB)
                        turn_rows(xn_part, i - 1)
                    if j == 3 and live(b, -1, B):
                        if i < DC:
                            query(i)
                        for m in MEM_BESIDE[i]:
                            turn_mem(b + 1, (par + 1) % 2, m)

                copied = []
                if live(t, 2, NT):
                    pe.wait_ge(s_masked, t * 2 - 3)
                    copied = [turn_prob(g) for g in GROUPS[:2]]
                if live(t, 3, NT):
                    pe.wait_ge(s_turnread, attT_copied)
                    if since(t, 4):
                        pe.wait_ge(s_res, t - 3)
                    product(outP[:, 0:D], [(attT[:, k, :], Cvo[:, k, :]) for k in range(DC)]).then_inc(s_proj, 1)
                if live(t, 2, NT):
                    mq = par if j >= 2 else (par + 1) % 2
                    if since(t, 3):
                        pe.wait_ge(s_att, t - 2)
                for i, g in enumerate(GROUPS):
                    if live(t, 2, NT):
                        pe.wait_ge(s_turnread, copied[i])
                        for c in g:
                            mm = pe.matmul(pvP[:, 0:D + 1], probT[0:rows(c), c, :], mem[0:rows(c), mq, c, :],
                                           start=(c == 0), stop=(c == SC - 1))
                        if i == NG - 1:
                            mm.then_inc(s_pv, 1)
                        if i + 2 < NG:
                            if i == 0:
                                pe.wait_ge(s_masked, t * 2 - 2)
                            copied.append(turn_prob(GROUPS[i + 2]))
                    beside(i)
                if j == 2 and live(b, 2, B):
                    pe.wait_ge(s_route, b * RK - 2 * RK + 15)
                    pe.wait_ge(s_cum, b * 5 - 9 + TPB)
                    product(give()[:, 0:TPB * E],
                            [(before[:], chosen[:].rearrange("p j e -> p (j e)")),
                             (ones[:], cum[:, 0:TPB, :].rearrange("p j e -> p (j e)"))]).then_inc(s_turn, 1)
                if isinstance(b, int) and b == B + 1 and j == 2:
                    pe.wait_ge(s_score, 2 * NT)
                    pe.wait_ge(s_cum, 5 * B - 4 + TPB)
                    product(scoreP[:, 0:E], [(ones[:], cum[:, TPB, :])]).then_inc(s_count, 1)
                if j == 3 and live(b, -1, B):
                    for m in MEM_LATE:
                        turn_mem(b + 1, (par + 1) % 2, m)

            walk(pe, step, turn)

            pe.wait_ge(s_turnread, turn.now())
            pe.wait_ge(s_plan, TILES_MADE)
            for k in range(2):
                for c in range(TC):
                    mm = pe.matmul(scoreP[0:1, 512 * (k + 1) + c * P:512 * (k + 1) + (c + 1) * P], tile_plan[:, k, c:c + 1],
                                   ident[:], start=True, stop=True)
            mm.then_inc(s_tiles, 1)
            pe.wait_ge(s_plan, TILES_PLANNED)
            pe.wait_ge(s_res, NT)
            pe.wait_ge(s_late, LATE_LOADS * 16)

            expert = {}

            def know(i, r, lag):
                if live(i, lag, MT) and r - lag not in expert:
                    expert[r - lag] = pe.value_load(tile_expert[0:1, bass.ds(i - lag, 1)], min_val=0, max_val=E - 1)

            def estep(i, r):
                if r == 0:
                    expert.clear()
                    know(i, r, 2)
                    know(i, r, 4)
                if live(i, 2, MT):
                    q = r % 2
                    e_gu = expert[r - 2]
                    pe.wait_ge(s_eturnc, i - 1)
                    if since(i, 4):
                        pe.wait_ge(s_eh, i * 2 - 6)
                    product(guP[q][:, 0:2 * F], [(xinT[:, q, k, :], Wgu_sb[k][:, bass.ds(e_gu, 1), :]) for k in range(DC)]).then_inc(s_gu, 1)
                if r < BODY - 1:
                    know(i + 1, r + 1, 2)
                    know(i + 1, r + 1, 4)
                if live(i, 0, MT):
                    pe.wait_ge(s_ein[r % RING], (i - r % RING) * 2 + 16)
                    if since(i, 2):
                        pe.wait_ge(s_eturnc, i - 1)
                    for c in range(DC):
                        mm = pe.transpose(turnP[r % 2][:, c * P:(c + 1) * P], xin[:, r % RING, c * P:(c + 1) * P], ident[:])
                    mm.then_inc(s_eturn, 1)
                if live(i, 4, MT):
                    q = r % 2
                    pe.wait_ge(s_ehTc, i - 3)
                    if since(i, 6):
                        pe.wait_ge(s_y, i - 5)
                    product(yP[q][:, 0:D], [(ehidT[:, q, :], Wd_sb[:, bass.ds(expert[r - 4], 1), :])]).then_inc(s_ydone, 1)
                if live(i, 3, MT):
                    q = (r - 3) % 2
                    pe.wait_ge(s_eh, i * 2 - 4)
                    if since(i, 5):
                        pe.wait_ge(s_ehTc, i - 4)
                    pe.transpose(ehTP[q][:, 0:P], ehid[:, q, :], ident[:]).then_inc(s_ehT, 1)

            ewalk(pe, estep)

            pe.wait_ge(s_eturnc, MT)
            pe.wait_ge(s_eh, 2 * MT)
            pe.wait_ge(s_y, MT)
            pe.wait_ge(s_weights, NWEIGHTS)

            def turn_xn3(b):
                pe.wait_ge(s_xn3, b * TPB + TPB)
                if since(b, 1):
                    pe.wait_ge(s_turn3c, b * DC)
                for c in range(DC):
                    for n in range(TPB):
                        mm = pe.transpose(turnP[c][:, n * P:(n + 1) * P], xn_part(n, c), ident[:])
                    mm.then_inc(s_turn3, 1)

            def gate_up(b, q, h):
                if h == 0:
                    pe.wait_ge(s_turn3c, b * DC + DC)
                if since(b, 1):
                    pe.wait_ge(s_hid, b * 4 + 2 * h - 2)
                for w in range(2):
                    f = w * FS + h * P
                    mm = product(sguP[2 * h + w], [(Sgu_sb[:, k, f:f + P], xn3T[:, q, k, :]) for k in range(DC)])
                mm.then_inc(s_sgu, 1)

            def down(b):
                pe.wait_ge(s_hid, b * 4 + 4)
                if since(b, 1):
                    pe.wait_ge(s_shared, b * DC)
                for c, bank in enumerate(yP):
                    for m in range(2):
                        n = 2 * c + m
                        mm = product(bank[:, m * D:(m + 1) * D],
                                     [(hid[:, f, n * P:(n + 1) * P], Sd_sb[:, f, :]) for f in range(FC)])
                    mm.then_inc(s_sdown, 1)

            def sstep(b, q):
                if live(b, 0, B):
                    gate_up(b, q, 0)
                if live(b, 1, B):
                    down(b - 1)
                if live(b, -1, B):
                    turn_xn3(b + 1)
                if live(b, 0, B):
                    gate_up(b, q, 1)

            turn_xn3(0)
            swalk(pe, sstep)


_INS = ["x", "ctx_1024", "L0_xattn_Wq", "L0_xattn_bq", "L0_xattn_Wk", "L0_xattn_bk", "L0_xattn_Wv", "L0_xattn_bv",
        "L0_xattn_Wo", "L0_xattn_bo", "L0_ffn_Wr", "L0_ffn_Wg", "L0_ffn_Wu", "L0_ffn_Wd", "L0_ffn_Sg", "L0_ffn_Su", "L0_ffn_Sd"]


def kernel(**inputs):
    import numpy as _np
    import concourse.bacc as _bacc
    from concourse import mybir as _mybir
    from concourse.bass_utils import run_bass_kernel_spmd as _run

    nc = _bacc.Bacc("TRN2", target_bir_lowering=False, num_devices=1)
    arrays, args = {}, []
    for name in _INS:
        a = _np.ascontiguousarray(inputs[name])
        arrays[f"in_{name}_dram"] = a
        args.append(nc.dram_tensor(f"in_{name}_dram", a.shape, _mybir.dt.from_np(a.dtype), kind="ExternalInput").ap())
    shape = _np.shape(inputs["x"])
    args.append(nc.dram_tensor("out_0_dram", shape, _mybir.dt.float32, kind="ExternalOutput").ap())
    xattn_moe_kernel(nc, *args)
    r = _run(nc, [arrays], core_ids=[0])
    return r.results[0]["out_0_dram"]
```
